# Optimizing a Trainium2 kernel written in Bass

```python
import numpy as np
import jax
import jax.numpy as jnp

def _softmax(x, axis=-1):
    return jax.nn.softmax(x, axis=axis)

def _gelu(x):
    return jax.nn.gelu(x, approximate=True)

def _silu(x):
    return jax.nn.silu(x)

def _sigmoid(x):
    return jax.nn.sigmoid(x)

def _layernorm(x, axis=-1, eps=1e-05):
    m = jnp.mean(x, axis=axis, keepdims=True)
    v = jnp.var(x, axis=axis, keepdims=True)
    return (x - m) / jnp.sqrt(v + eps)

def _scatter_add(tgt, idx, src, axis=0):
    return tgt.at[idx].add(src)

def _segment_sum(src, seg, n):
    return jax.ops.segment_sum(src, seg, n)
kernel_name = 'mk_gnn_resnorm_d2_gnn_r8_bf14f5'

def setup_inputs(seed: int=0):
    np.random.seed(seed)
    _w = jnp.asarray

    def _rec_inputs():
        import jax
        import jax.numpy as jnp
        _gk = jax.random.key(seed)
        x = -6.415e-05 + 1 * jax.random.normal(jax.random.fold_in(_gk, 1), (1250, 512), jnp.float32)
        _s = jax.random.randint(jax.random.fold_in(_gk, 2), (10000,), 0, 1250, jnp.int32)
        _d = jax.random.randint(jax.random.fold_in(_gk, 3), (10000,), 0, 1250, jnp.int32)
        _loop = jnp.arange(1250, dtype=jnp.int32)
        src = jnp.concatenate([_s, _d, _loop])
        dst = jnp.concatenate([_d, _s, _loop])
        _o = jnp.argsort(dst, stable=True)
        src = src[_o]
        dst = dst[_o]
        edge_attr_4 = 0.000998654 + 0.999792 * jax.random.normal(jax.random.fold_in(_gk, 12), (21250, 4), jnp.float32)
        return (x, src, dst, edge_attr_4)
    x, src, dst, edge_attr_4 = _rec_inputs()

    def _L0_gnn_setup():
        import jax, jax.numpy as jnp
        import numpy as np
        N_NODES = 2500
        N_EDGES = 40000
        D = 512
        L = 3
        key = jax.random.key(seed)
        ks = jax.random.split(key, 6)
        x = jax.random.normal(ks[0], (N_NODES, D), dtype=jnp.float32)
        Ws_self = jax.random.normal(ks[1], (L, D, D), dtype=jnp.float32) * 0.05
        Ws_neigh = jax.random.normal(ks[2], (L, D, D), dtype=jnp.float32) * 0.05
        bs = jax.random.normal(ks[3], (L, D), dtype=jnp.float32) * 0.05
        src = jax.random.randint(ks[4], (N_EDGES,), 0, N_NODES, dtype=jnp.int64)
        dst = jax.random.randint(ks[5], (N_EDGES,), 0, N_NODES, dtype=jnp.int64)
        return {'x': x, 'Ws_self': Ws_self, 'Ws_neigh': Ws_neigh, 'bs': bs, 'src': src, 'dst': dst}
    _L0_gnn_all = _L0_gnn_setup()
    _L0_gnn_in = {k: v for k, v in _L0_gnn_all.items() if k in ('Ws_self', 'Ws_neigh', 'bs')}
    del _L0_gnn_all

    def _L1_gnn_setup():
        import jax, jax.numpy as jnp
        import numpy as np
        EPS = 1e-05

        def _ln(x, g, b):
            m = x.mean(-1, keepdims=True)
            v = ((x - m) ** 2).mean(-1, keepdims=True)
            return (x - m) / jnp.sqrt(v + EPS) * g + b

        def _mlp(x, W0, b0, W1, b1, g, b):
            h = jax.nn.silu(x @ W0 + b0)
            return _ln(h @ W1 + b1, g, b)
        NG, NM, E, D, H = (8192, 40962, 24576, 512, 512)
        key = jax.random.key(seed)
        ks = jax.random.split(key, 16)

        def lin(k, i, o):
            return (jax.random.normal(k, (i, o), jnp.float32) / np.sqrt(i)).astype(jnp.float32)
        inp = {'grid_nfeat': jax.random.normal(ks[0], (NG, D), jnp.float32), 'mesh_nfeat': jax.random.normal(ks[1], (NM, D), jnp.float32), 'edge_index': jax.random.randint(ks[2], (2, E), 0, NM), 'mesh2grid_efeat': jax.random.normal(ks[3], (E, 4), jnp.float32), 'emb_W0': lin(ks[4], 4, H), 'emb_b0': jnp.zeros(H, jnp.float32), 'emb_W1': lin(ks[5], H, D), 'emb_b1': jnp.zeros(D, jnp.float32), 'emb_g': jnp.ones(D, jnp.float32), 'emb_b': jnp.zeros(D, jnp.float32), 'edge_W0': lin(ks[6], 3 * D, H), 'edge_b0': jnp.zeros(H, jnp.float32), 'edge_W1': lin(ks[7], H, D), 'edge_b1': jnp.zeros(D, jnp.float32), 'edge_g': jnp.ones(D, jnp.float32), 'edge_beta': jnp.zeros(D, jnp.float32), 'node_W0': lin(ks[8], 2 * D, H), 'node_b0': jnp.zeros(H, jnp.float32), 'node_W1': lin(ks[9], H, D), 'node_b1': jnp.zeros(D, jnp.float32), 'node_g': jnp.ones(D, jnp.float32), 'node_beta': jnp.zeros(D, jnp.float32)}
        return inp
    _L1_gnn_all = _L1_gnn_setup()
    _L1_gnn_in = {k: v for k, v in _L1_gnn_all.items() if k in ('mesh_nfeat', 'emb_W0', 'emb_b0', 'emb_W1', 'emb_b1', 'emb_g', 'emb_b', 'edge_W0', 'edge_b0', 'edge_W1', 'edge_b1', 'edge_g', 'edge_beta', 'node_W0', 'node_b0', 'node_W1', 'node_b1', 'node_g', 'node_beta')}
    del _L1_gnn_all
    return {'x': x, 'src': src, 'dst': dst, 'edge_attr_4': edge_attr_4, 'L0_gnn_Ws_self': _L0_gnn_in['Ws_self'], 'L0_gnn_Ws_neigh': _L0_gnn_in['Ws_neigh'], 'L0_gnn_bs': _L0_gnn_in['bs'], 'L1_gnn_mesh_nfeat': _L1_gnn_in['mesh_nfeat'], 'L1_gnn_emb_W0': _L1_gnn_in['emb_W0'], 'L1_gnn_emb_b0': _L1_gnn_in['emb_b0'], 'L1_gnn_emb_W1': _L1_gnn_in['emb_W1'], 'L1_gnn_emb_b1': _L1_gnn_in['emb_b1'], 'L1_gnn_emb_g': _L1_gnn_in['emb_g'], 'L1_gnn_emb_b': _L1_gnn_in['emb_b'], 'L1_gnn_edge_W0': _L1_gnn_in['edge_W0'], 'L1_gnn_edge_b0': _L1_gnn_in['edge_b0'], 'L1_gnn_edge_W1': _L1_gnn_in['edge_W1'], 'L1_gnn_edge_b1': _L1_gnn_in['edge_b1'], 'L1_gnn_edge_g': _L1_gnn_in['edge_g'], 'L1_gnn_edge_beta': _L1_gnn_in['edge_beta'], 'L1_gnn_node_W0': _L1_gnn_in['node_W0'], 'L1_gnn_node_b0': _L1_gnn_in['node_b0'], 'L1_gnn_node_W1': _L1_gnn_in['node_W1'], 'L1_gnn_node_b1': _L1_gnn_in['node_b1'], 'L1_gnn_node_g': _L1_gnn_in['node_g'], 'L1_gnn_node_beta': _L1_gnn_in['node_beta']}

def reference(x, src, dst, edge_attr_4, L0_gnn_Ws_self, L0_gnn_Ws_neigh, L0_gnn_bs, L1_gnn_mesh_nfeat, L1_gnn_emb_W0, L1_gnn_emb_b0, L1_gnn_emb_W1, L1_gnn_emb_b1, L1_gnn_emb_g, L1_gnn_emb_b, L1_gnn_edge_W0, L1_gnn_edge_b0, L1_gnn_edge_W1, L1_gnn_edge_b1, L1_gnn_edge_g, L1_gnn_edge_beta, L1_gnn_node_W0, L1_gnn_node_b0, L1_gnn_node_W1, L1_gnn_node_b1, L1_gnn_node_g, L1_gnn_node_beta):
    import jax
    import jax.numpy as jnp

    def _L0_gnn_ref(x, Ws_self, Ws_neigh, bs, src, dst):
        import jax, jax.numpy as jnp
        import numpy as np
        N_NODES = 2500
        N_EDGES = 40000
        D = 512
        L = 3
        n = x.shape[0]
        deg = jax.ops.segment_sum(jnp.ones_like(dst, dtype=x.dtype), dst, num_segments=n)
        inv_deg = (1.0 / jnp.clip(deg, 1.0))[:, None]
        h = x
        n_layers = Ws_self.shape[0]
        for l in range(n_layers):
            neigh = jax.ops.segment_sum(h[src], dst, num_segments=n) * inv_deg
            h = h @ Ws_self[l] + neigh @ Ws_neigh[l] + bs[l]
            if l != n_layers - 1:
                h = jax.nn.relu(h)
        return h

    def _L1_gnn_ref(grid_nfeat, mesh_nfeat, edge_index, mesh2grid_efeat, emb_W0, emb_b0, emb_W1, emb_b1, emb_g, emb_b, edge_W0, edge_b0, edge_W1, edge_b1, edge_g, edge_beta, node_W0, node_b0, node_W1, node_b1, node_g, node_beta):
        import jax, jax.numpy as jnp
        import numpy as np
        EPS = 1e-05

        def _ln(x, g, b):
            m = x.mean(-1, keepdims=True)
            v = ((x - m) ** 2).mean(-1, keepdims=True)
            return (x - m) / jnp.sqrt(v + EPS) * g + b

        def _mlp(x, W0, b0, W1, b1, g, b):
            h = jax.nn.silu(x @ W0 + b0)
            return _ln(h @ W1 + b1, g, b)
        NG, NM, E, D, H = (8192, 40962, 24576, 512, 512)
        e = _mlp(mesh2grid_efeat, emb_W0, emb_b0, emb_W1, emb_b1, emb_g, emb_b)
        src = edge_index[0]
        dst = edge_index[1]
        e_in = jnp.concatenate([e, mesh_nfeat[src], grid_nfeat[dst]], axis=-1)
        e_new = _mlp(e_in, edge_W0, edge_b0, edge_W1, edge_b1, edge_g, edge_beta) + e
        agg = jax.ops.segment_sum(e_new, dst, num_segments=grid_nfeat.shape[0])
        n_in = jnp.concatenate([grid_nfeat, agg], axis=-1)
        n_new = _mlp(n_in, node_W0, node_b0, node_W1, node_b1, node_g, node_beta) + grid_nfeat
        return n_new
    edge_index = jnp.stack([src, dst])
    x = _layernorm(x + _L0_gnn_ref(x, L0_gnn_Ws_self, L0_gnn_Ws_neigh, L0_gnn_bs, src, dst), axis=-1)
    x = _layernorm(x + _L1_gnn_ref(x, L1_gnn_mesh_nfeat, edge_index, edge_attr_4, L1_gnn_emb_W0, L1_gnn_emb_b0, L1_gnn_emb_W1, L1_gnn_emb_b1, L1_gnn_emb_g, L1_gnn_emb_b, L1_gnn_edge_W0, L1_gnn_edge_b0, L1_gnn_edge_W1, L1_gnn_edge_b1, L1_gnn_edge_g, L1_gnn_edge_beta, L1_gnn_node_W0, L1_gnn_node_b0, L1_gnn_node_W1, L1_gnn_node_b1, L1_gnn_node_g, L1_gnn_node_beta), axis=-1)
    return x

_drawn_inputs = setup_inputs


def setup_inputs(seed=0):
    import zlib

    import numpy as np

    out = dict(_drawn_inputs(seed))
    spreads = {'L1_gnn_emb_b0': (0.0, 0.1),
     'L1_gnn_emb_b1': (0.0, 0.1),
     'L1_gnn_emb_g': (1.0, 0.2),
     'L1_gnn_emb_b': (0.0, 0.1),
     'L1_gnn_edge_b0': (0.0, 0.1),
     'L1_gnn_edge_b1': (0.0, 0.1),
     'L1_gnn_edge_g': (1.0, 0.2),
     'L1_gnn_edge_beta': (0.0, 0.1),
     'L1_gnn_node_b0': (0.0, 0.8),
     'L1_gnn_node_b1': (0.0, 0.8),
     'L1_gnn_node_g': (1.0, 0.2),
     'L1_gnn_node_beta': (0.0, 0.1)}
    factors = {}
    for name, (base, spread) in spreads.items():
        noise = np.random.default_rng([zlib.crc32(name.encode()), seed]).standard_normal(out[name].shape)
        drawn = base * np.exp(spread * noise) if base else spread * noise
        out[name] = jnp.asarray(drawn.astype(out[name].dtype))
    for name, factor in factors.items():
        out[name] = (out[name] * factor).astype(out[name].dtype)
    return out
```

```python
from contextlib import ExitStack

import concourse.bass as bass
from concourse import mybir

F32 = mybir.dt.float32
F32R = mybir.dt.float32r
BF16 = mybir.dt.bfloat16
I32 = mybir.dt.int32
I16 = mybir.dt.int16
ALU = mybir.AluOpType
ACT = mybir.ActivationFunctionType
AX = mybir.AxisListType
ds = bass.ds

P = 128
N = 1250
E = 21250
D = 512
A4 = 4
KC = D // P
NB = 10
NPB = N // NB
EP, EC = 125, E // 125
TILES = (E + NB * P) // P
REC = 8
F_DST, F_SRC, F_DSTG, F_ATTR = 0, 1, 2, 3
STK = 32
EPS = 1e-5
SCAT = 17
GROUP = 4
GROUPS = TILES // GROUP
SQUARE_BLOCKS = (slice(0, 3), slice(1, 4), slice(2, 4), slice(0, 4, 3))
assert TILES % GROUP == 0 and EC % (2 * SCAT) == 0 and NPB * NB == N and EP * EC == E


def product(pe, out, lhs, rhs, chunks):
    for i, k in enumerate(chunks):
        pe.matmul(out, lhs[0](k), rhs[0](k), start=(i == 0), stop=False, skip_group_check=True)
        pe.matmul(out, lhs[0](k), rhs[1](k), start=False, stop=False, skip_group_check=True)
        last = pe.matmul(out, lhs[1](k), rhs[0](k), start=False, stop=(i == len(chunks) - 1),
                         skip_group_check=True)
    return last


class Chain:

    def __init__(self, engine, sem):
        self.engine, self.sem, self.n = engine, sem, 0

    def after(self, ins):
        self.n += 1
        ins.then_inc(self.sem, 1)
        self.engine.wait_ge(self.sem, self.n)


def rows(vector):
    return vector.rearrange("(a n) -> a n", a=1)


def columns(vector):
    return vector.rearrange("(k p) -> p k", p=P)


def chunked(matrix):
    return matrix.rearrange("(k p) n -> p k n", p=P)


def phase_a(nc, ctx, t, scratch, keep):
    def sb(name, shape, dt=F32):
        return ctx.enter_context(nc.sbuf_tensor("a_" + name, shape, dt))

    def sem(name):
        semaphores.append(nc.alloc_semaphore("a_" + name))
        return semaphores[-1]

    semaphores = []

    bank = [ctx.enter_context(nc.psum_tensor(f"a_bank{i}", [P, 512], F32)) for i in range(8)]
    src_i, dst_i = sb("src_i", [EP, EC], I32), sb("dst_i", [EP, EC], I32)
    attr_in = sb("attr_in", [EP, EC * A4])
    dst_f, bucket, where, part = (sb(n, [EP, EC]) for n in ("dst_f", "bucket", "where", "part"))
    zero = sb("zero", [EP, EC])
    mask, scan = sb("mask", [EP, NB, EC]), sb("scan", [EP, NB, EC])
    totals, offset = sb("totals", [EP, NB]), sb("offset", [EP, NB])
    slot_i, slot_lo, slot_hi = (sb(n, [EP, EC], I32) for n in ("slot_i", "slot_lo", "slot_hi"))
    row_i = sb("row_i", [EP, EC], I32)
    record = sb("record", [EP, EC, REC])
    counts, tiles_f, ends, starts = (sb(n, [P, NB]) for n in ("counts", "tiles_f", "ends", "starts"))
    counts_i, ends_i = sb("counts_i", [P, NB], I32), sb("ends_i", [P, NB], I32)
    tile_no, tile_bucket = sb("tile_no", [P, TILES + 1]), sb("tile_bucket", [P, TILES + 1])
    tile_step, tile_flag = sb("tile_step", [P, TILES]), sb("tile_flag", [P, TILES])
    before, ones = sb("before", [P, P]), sb("ones", [P, P])
    pads = sb("pads", [P, TILES * REC])
    stage_row = [sb(f"stage_row{i}", [EP, SCAT], I32) for i in range(2)]
    stage_rec = [sb(f"stage_rec{i}", [EP, SCAT, REC]) for i in range(2)]
    w1 = [sb(f"w1_{i}", [P, KC, D]) for i in range(2)]
    w1t = [sb(f"w1t_{i}", [P, KC, D]) for i in range(2)]
    w1gt = [sb(f"w1gt_{i}", [P, KC, D]) for i in range(2)]
    w0a, w0b, wnb = (sb(n, [P, KC, D]) for n in ("w0a", "w0b", "wnb"))
    vecs = [sb(f"vecs_{i}", [P, 3, KC]) for i in range(2)]
    cols = [sb(f"cols_{i}", [P, 4, KC]) for i in range(2)]
    shift_sum = sb("shift_sum", [P, KC])
    mean = sb("mean", [P, 2, KC])
    bsum = sb("bsum", [P, 2])
    jobs_out = [sb(f"jobs_out{i}", [P, D]) for i in range(2)]
    rows_out = [sb(f"rows_out{i}", [1, D]) for i in range(2)]
    mesh = [sb(f"mesh{i}", [NPB, D]) for i in range(2)]
    mesh_t = [sb(f"mesh_t{i}", [P, KC, P]) for i in range(2)]
    mesh_out = [sb(f"mesh_out{i}", [NPB, D]) for i in range(2)]
    src_grid, dst_grid = sb("src_grid", [P, NB * P], I16), sb("dst_grid", [P, P], I16)
    hot_src = [sb(f"hot_src{i}", [P, NB * P], BF16) for i in range(2)]
    hot_dst = [sb(f"hot_dst{i}", [P, P], BF16) for i in range(2)]
    ones16, zeros16 = sb("ones16", [P, 2], BF16), sb("zeros16", [P, 512], BF16)
    k, recs = keep, keep["recs"]

    edges_in, weights_in, vecs_in = sem("edges_in"), sem("weights_in"), sem("vecs_in")
    pool_const, dve_const = sem("pool_const"), sem("dve_const")
    pads_out, dve_chain = sem("pads_out"), sem("dve_chain")
    totals_ok, totals_mm, rows_ok, tables_ok = (sem(n) for n in ("totals_ok", "totals_mm", "rows_ok", "tables_ok"))
    staged, tick = sem("staged"), sem("tick")
    scattered = [sem(f"scattered{i}") for i in range(2)]
    recs_in = sem("recs_in")
    centred, turned, turned_out, gains_ok, bias_mm, cols_ok = (
        sem(n) for n in ("centred", "turned", "turned_out", "gains_ok", "bias_mm", "cols_ok"))
    job_mm, job_copied, job_out_ok, square_mm = (sem(n) for n in ("job_mm", "job_copied", "job_out_ok", "square_mm"))
    row_out_ok = sem("row_out_ok")
    job_out = [sem(f"job_out{i}") for i in range(2)]
    mesh_in = [sem(f"mesh_in{i}") for i in range(2)]
    mesh_stored = [sem(f"mesh_stored{i}") for i in range(2)]
    mesh_turned, mesh_t_ok, mesh_mm, mesh_ok = (sem(n) for n in ("mesh_turned", "mesh_t_ok", "mesh_mm", "mesh_ok"))
    hot_ok, count_mm, counts_out = sem("hot_ok"), sem("count_mm"), sem("counts_out")
    counts_copied, wiped = sem("counts_copied"), sem("wiped")

    matrices = [("square1", w1t[0], w1t[0]), ("fold_edge", w1gt[0], w0a), ("square2", w1t[1], w1t[1]),
                ("fold_node1", w1gt[0], wnb), ("fold_node2", w1gt[1], wnb)]
    vectors = [("lin1", cols[0][:, 0], w1t[0]), ("fold_edge_b", cols[0][:, 1], w0a), ("lin2", cols[1][:, 0], w1t[1]),
               ("edge_shift", cols[0][:, 2], w0a), ("node_r1", cols[0][:, 1], wnb),
               ("node_r2", cols[1][:, 1], wnb), ("node_count", shift_sum, wnb)]
    NJ = len(matrices) * KC

    ctx.callback(nc.all_engine_barrier)
    ctx.callback(lambda: nc.clear_and_free_semaphores(semaphores))
    block = ctx.enter_context(nc.Block())

    @block.sync
    def _(sp):
        sp.dma_start(dst_i[:], t["dst"].rearrange("(p j) -> p j", p=EP)).then_inc(edges_in, 16)
        sp.dma_start(src_i[:], t["src"].rearrange("(p j) -> p j", p=EP)).then_inc(edges_in, 16)
        sp.dma_start(attr_in[:], t["edge_attr_4"].rearrange("(p j) a -> p (j a)", p=EP)).then_inc(edges_in, 16)
        sp.wait_ge(dve_const, 3)
        sp.dma_start(scratch["records"].rearrange("(p t) f -> p (t f)", p=P), pads[:]).then_inc(pads_out, 16)
        sp.dma_start(w1[0][:], chunked(t["L1_gnn_emb_W1"])).then_inc(weights_in, 16)
        sp.dma_start(w1[1][:], chunked(t["L1_gnn_edge_W1"])).then_inc(weights_in, 16)
        sp.dma_start(w0a[:], chunked(t["L1_gnn_edge_W0"][0:D, :])).then_inc(weights_in, 16)
        sp.dma_start(w0b[:], chunked(t["L1_gnn_edge_W0"][D:2 * D, :])).then_inc(weights_in, 16)
        sp.dma_start(wnb[:], chunked(t["L1_gnn_node_W0"][D:2 * D, :])).then_inc(weights_in, 16)
        for i, names in enumerate((("emb_b1", "emb_g", "emb_b"), ("edge_b1", "edge_g", "edge_beta"))):
            for j, name in enumerate(names):
                sp.dma_start(vecs[i][:, j, :], columns(t["L1_gnn_" + name]),
                             allow_slow_non_contiguous=True).then_inc(vecs_in, 16)
        for n in range(2):
            sp.dma_start(mesh[n][:], t["L1_gnn_mesh_nfeat"][n * NPB:(n + 1) * NPB, :]).then_inc(mesh_in[n], 16)
        for j in range(NJ):
            name, i = matrices[j // KC][0], j % KC
            sp.wait_ge(job_out_ok, j + 1)
            sp.dma_start(scratch[name][i * P:(i + 1) * P, :], jobs_out[j % 2][:]).then_inc(job_out[j % 2], 16)
        for r in range(len(vectors)):
            sp.wait_ge(row_out_ok, r + 1)
            sp.dma_start(rows(scratch[vectors[r][0]]), rows_out[r % 2][:]).then_inc(job_out[r % 2], 16)
        with sp.Fori(0, NB // 2 - 1) as i:
            for u in range(2):
                sp.wait_ge(mesh_turned, 2 * i + u + 1)
                sp.dma_start(mesh[u][:], t["L1_gnn_mesh_nfeat"][ds((2 * i + 2 + u) * NPB, NPB), :]).then_inc(mesh_in[u], 16)
            for u in range(2):
                sp.wait_ge(mesh_ok, 2 * i + u + 1)
                sp.dma_start(scratch["mesh_table"][ds((2 * i + u) * NPB, NPB), :], mesh_out[u][:]).then_inc(mesh_stored[u], 16)
        for u in range(2):
            n = NB - 2 + u
            sp.wait_ge(mesh_ok, n + 1)
            sp.dma_start(scratch["mesh_table"][n * NPB:(n + 1) * NPB, :], mesh_out[u][:]).then_inc(mesh_stored[u], 16)
        for u in range(2):
            sp.wait_ge(scattered[u], 16 * EC // 2)
        sp.dma_start(recs[:], scratch["records"].rearrange("(p t) f -> p t f", p=P)).then_inc(recs_in, 16)
        for u in range(2):
            sp.wait_ge(job_out[u], 16 * (NJ // 2) + 16 * ((len(vectors) + 1 - u) // 2))
            sp.wait_ge(mesh_stored[u], 16 * NB // 2)

    @block.gpsimd
    def _(pool):
        pool.iota(dst_grid[:], [[1, P]], base=0, channel_multiplier=0).then_inc(pool_const, 1)
        pool.iota(src_grid[:], [[NPB, NB], [1, P]], base=0, channel_multiplier=0).then_inc(pool_const, 1)
        pool.iota(tile_no[:], [[1, TILES + 1]], base=0, channel_multiplier=0,
                  allow_small_or_imprecise_dtypes=True).then_inc(pool_const, 1)
        pool.iota(k["grid"][:], [[1, P]], base=0, channel_multiplier=0,
                  allow_small_or_imprecise_dtypes=True).then_inc(pool_const, 1)
        pool.wait_ge(dve_const, 2)
        pool.affine_select(out=k["ident"][:], in_=k["ident"][:], compare_op=ALU.not_equal, fill=1.0, base=0,
                           pattern=[[-1, P]], channel_multiplier=1).then_inc(pool_const, 1)
        pool.affine_select(out=before[:], in_=before[:], compare_op=ALU.is_gt, fill=0.0, base=0,
                           pattern=[[1, P]], channel_multiplier=-1).then_inc(pool_const, 1)
        def stage(u, j, fixed):
            at = slice((2 * j + u) * SCAT, (2 * j + u + 1) * SCAT) if fixed else ds((2 * j + u) * SCAT, SCAT)
            if not fixed:
                pool.wait_ge(scattered[u], j * (16 * SCAT))
                pool.sem_inc(tick, 1)
            pool.tensor_copy(stage_row[u][:], row_i[:, at]).then_inc(staged, 1)
            pool.tensor_copy(stage_rec[u][:], record[:, at, :]).then_inc(staged, 1)
            pool.wait_ge(staged, (2 * j + u + 1) * 2)
            if not fixed:
                pool.sem_inc(tick, 1)
            for c in range(SCAT):
                pool.indirect_dma_start(scratch["records"], bass.IndirectOffsetOnAxis(ap=stage_row[u][:, c:c + 1], axis=0),
                                        stage_rec[u][:, c, :], None).then_inc(scattered[u], 16)

        pool.wait_ge(pads_out, 16)
        pool.wait_ge(rows_ok, 1)
        for u in range(2):
            stage(u, 0, True)
        with pool.Fori(1, EC // (2 * SCAT)) as j:
            for u in range(2):
                stage(u, j, False)

    @block.vector
    def _(dve):
        chain = Chain(dve, dve_chain)
        dve.memset(k["ident"][:], 0.0).then_inc(dve_const, 1)
        dve.memset(before[:], 1.0).then_inc(dve_const, 1)
        chain.after(dve.memset(pads[:], 0.0))
        dve.memset(pads[:].rearrange("p (t f) -> p t f", f=REC)[:, :, F_DST:F_DST + 1], -1.0).then_inc(dve_const, 1)
        dve.memset(ones[:], 1.0).then_inc(dve_const, 1)
        dve.memset(ones16[:], 1.0).then_inc(dve_const, 1)
        dve.memset(zeros16[:], 0.0).then_inc(dve_const, 1)
        dve.memset(zero[:], 0.0)
        dve.memset(record[:, :, F_ATTR + A4:], 0.0)
        dve.memset(k["half"][:], -0.5)
        dve.memset(k["zeros"][:], 0.0)
        dve.wait_ge(edges_in, 48)
        chain.after(dve.tensor_copy(dst_f[:], dst_i[:]))
        dve.tensor_copy(record[:, :, F_SRC], src_i[:])
        dve.tensor_copy(record[:, :, F_ATTR:F_ATTR + A4], attr_in[:].rearrange("p (j a) -> p j a", a=A4))
        dve.tensor_copy(record[:, :, F_DSTG], dst_f[:])
        chain.after(dve.tensor_scalar(bucket[:], dst_f[:], float(NPB), None, ALU.is_ge))
        for c in range(2, NB):
            chain.after(dve.scalar_tensor_tensor(out=bucket[:], in0=dst_f[:], scalar=float(c * NPB), in1=bucket[:],
                                                 op0=ALU.is_ge, op1=ALU.add))
        dve.scalar_tensor_tensor(out=record[:, :, F_DST], in0=bucket[:], scalar=-float(NPB), in1=dst_f[:],
                                 op0=ALU.mult, op1=ALU.add)
        for c in range(NB):
            last = dve.tensor_scalar(mask[:, c, :], bucket[:], float(c), None, ALU.is_equal)
        chain.after(last)
        for c in range(NB):
            last = dve.tensor_tensor_scan(out=scan[:, c, :], data0=mask[:, c, :], data1=zero[:], initial=0.0,
                                          op0=ALU.add, op1=ALU.add)
        chain.after(last)
        dve.tensor_copy(totals[:], scan[:, :, EC - 1]).then_inc(totals_ok, 1)
        dve.wait_ge(totals_mm, 1)
        chain.after(dve.tensor_scalar(counts[:], bank[1][:, 0:NB], float(P - 1), None, ALU.add))
        chain.after(dve.tensor_copy(counts_i[:], counts[:]))
        chain.after(dve.tensor_scalar(counts_i[:], counts_i[:], 7, None, ALU.logical_shift_right))
        chain.after(dve.tensor_copy(tiles_f[:], counts_i[:]))
        chain.after(dve.tensor_scalar(tiles_f[:], tiles_f[:], 1.0, None, ALU.max))
        chain.after(dve.tensor_tensor_scan(out=ends[:], data0=tiles_f[:], data1=k["zeros"][:, 0:NB],
                                           initial=0.0, op0=ALU.add, op1=ALU.add))
        chain.after(dve.tensor_tensor(starts[:], ends[:], tiles_f[:], ALU.subtract))
        chain.after(dve.tensor_scalar(offset[:], starts[0:EP, :], float(P), -1.0, ALU.mult, ALU.add))
        chain.after(dve.tensor_tensor(offset[:], offset[:], bank[0][0:EP, 0:NB], ALU.add))
        for c in range(NB):
            to = where if c == 0 else part
            chain.after(dve.scalar_tensor_tensor(out=to[:], in0=scan[:, c, :], scalar=offset[:, c:c + 1], in1=mask[:, c, :],
                                                 op0=ALU.add, op1=ALU.mult))
            if c:
                chain.after(dve.tensor_tensor(where[:], where[:], part[:], ALU.add))
        chain.after(dve.tensor_copy(slot_i[:], where[:]))
        dve.tensor_scalar(slot_lo[:], slot_i[:], P - 1, None, ALU.bitwise_and)
        chain.after(dve.tensor_scalar(slot_hi[:], slot_i[:], 7, None, ALU.logical_shift_right))
        chain.after(dve.scalar_tensor_tensor(out=row_i[:], in0=slot_lo[:], scalar=float(TILES), in1=slot_hi[:],
                                             op0=ALU.mult, op1=ALU.add))
        dve.sem_inc(rows_ok, 1)
        dve.wait_ge(pool_const, 6)
        chain.after(dve.tensor_scalar(tile_bucket[:], tile_no[:], starts[:, 1:2], None, ALU.is_ge))
        for c in range(2, NB):
            chain.after(dve.scalar_tensor_tensor(out=tile_bucket[:], in0=tile_no[:], scalar=starts[:, c:c + 1], in1=tile_bucket[:],
                                                 op0=ALU.is_ge, op1=ALU.add))
        dve.memset(tile_bucket[:, TILES:], float(NB))
        chain.after(dve.tensor_copy(ends_i[:], ends[:]))
        chain.after(dve.tensor_tensor(tile_step[:], tile_bucket[:, 1:], tile_bucket[:, :TILES], ALU.subtract))
        chain.after(dve.scalar_tensor_tensor(out=tile_flag[:], in0=tile_bucket[:, :TILES], scalar=1.0, in1=tile_step[:],
                                             op0=ALU.add, op1=ALU.mult))
        dve.tensor_copy(k["tile_last"][:], tile_flag[:])
        dve.tensor_scalar(k["tile_bucket1"][:], tile_bucket[:, :TILES], 1.0, None, ALU.add)
        dve.tensor_copy(k["bucket_end"][:], ends_i[:]).then_inc(tables_ok, 1)
        dve.wait_ge(weights_in, 80)
        dve.wait_ge(vecs_in, 96)
        for i in range(2):
            chain.after(dve.tensor_reduce(mean[:, i, :], w1[i][:], AX.X, ALU.add))
            chain.after(dve.tensor_scalar(mean[:, i, :], mean[:, i, :], 1.0 / D, None, ALU.mult))
            for c in range(KC):
                last = dve.tensor_scalar(w1[i][:, c, :], w1[i][:, c, :], mean[:, i, c:c + 1], None, ALU.subtract)
            last.then_inc(centred, 1)
            chain.after(dve.tensor_reduce(bsum[:, i:i + 1], vecs[i][:, 0, :], AX.X, ALU.add))
        dve.sem_inc(centred, 1)
        dve.wait_ge(bias_mm, 1)
        chain.after(dve.tensor_scalar(bsum[:], bank[2][:, 0:2], 1.0 / D, None, ALU.mult))
        for i in range(2):
            chain.after(dve.tensor_scalar(vecs[i][:, 0, :], vecs[i][:, 0, :], bsum[:, i:i + 1], None, ALU.subtract))
            dve.tensor_scalar(cols[i][:, 0, :], vecs[i][:, 0, :], 2.0, None, ALU.mult)
            dve.tensor_tensor(cols[i][:, 1, :], vecs[i][:, 0, :], vecs[i][:, 1, :], ALU.mult)
            dve.tensor_copy(cols[i][:, 2, :], vecs[i][:, 2, :])
            dve.tensor_tensor(cols[i][:, 3, :], vecs[i][:, 0, :], vecs[i][:, 0, :], ALU.mult)
        dve.tensor_tensor(shift_sum[:], vecs[0][:, 2, :], vecs[1][:, 2, :], ALU.add).then_inc(cols_ok, 1)
        for i in range(2):
            for o in range(KC):
                dve.wait_ge(turned, KC * i + o + 1)
                chain.after(dve.tensor_copy(w1t[i][:, o, :], bank[4 + o][:]))
                dve.sem_inc(turned_out, 1)
                last = dve.tensor_scalar(w1gt[i][:, o, :], w1t[i][:, o, :], vecs[i][:, 1, o:o + 1], None, ALU.mult)
            last.then_inc(gains_ok, 1)
        dve.wait_ge(square_mm, 1)
        dve.tensor_scalar(k["floor"][:], bank[3][:, 0:2], 1.0 / D, EPS, ALU.mult, ALU.add).then_inc(dve_const, 1)
        def mesh_copy(n, u, fixed):
            if not fixed:
                dve.wait_ge(mesh_stored[u], (n - u) * 8)
            dve.wait_ge(mesh_mm, n + 1)
            dve.tensor_copy(mesh_out[u][:], bank[6 + u][0:NPB, :]).then_inc(mesh_ok, 1)

        for u in range(2):
            mesh_copy(u, u, True)
        with dve.Fori(1, NB // 2) as i:
            for u in range(2):
                mesh_copy(2 * i + u, u, False)
        dve.wait_ge(recs_in, 16)
        def field(n, f):
            return recs[:, n, f:f + 1] if isinstance(n, int) else recs[:, ds(n, 1), f:f + 1].rearrange("p a b -> p (a b)")

        def one_hot(n, u, fixed):
            if not fixed:
                dve.wait_ge(count_mm, n - 1)
            dve.tensor_scalar(hot_src[u][:], src_grid[:], field(n, F_SRC), None, ALU.is_equal)
            dve.tensor_scalar(hot_dst[u][:], dst_grid[:], field(n, F_DST), None, ALU.is_equal).then_inc(hot_ok, 1)

        for u in range(2):
            one_hot(u, u, True)
        with dve.Fori(1, TILES // 2) as i:
            for u in range(2):
                one_hot(2 * i + u, u, False)

    @block.scalar
    def _(act):
        for j in range(NJ):
            name, i = matrices[j // KC][0], j % KC
            act.wait_ge(job_mm, j + 1)
            if j >= 2:
                act.wait_ge(job_out[j % 2], 16 * (j // 2))
            if name.startswith("square"):
                for c in range(KC):
                    to = slice(c * P, (c + 1) * P)
                    last = act.activation(jobs_out[j % 2][:, to], bank[j % 2][:, to], ACT.Copy, scale=1.0 if c == i else 2.0)
            else:
                last = act.activation(jobs_out[j % 2][:], bank[j % 2][:], ACT.Copy)
            last.then_inc(job_out_ok, 1)
        for r in range(len(vectors)):
            act.wait_ge(job_mm, NJ + r + 1)
            act.wait_ge(job_out[r % 2], 16 * (NJ // 2) + 16 * (r // 2))
            act.activation(rows_out[r % 2][:], bank[r % 2][0:1, :], ACT.Copy).then_inc(row_out_ok, 1)
        def mesh_copy(n, u, fixed):
            if not fixed:
                act.wait_ge(mesh_mm, n - 1)
            act.wait_ge(mesh_turned, n + 1)
            act.activation(mesh_t[u][:, :, 0:NPB],
                           bank[4 + u][:].rearrange("p (k n) -> p k n", k=KC)[:, :, 0:NPB], ACT.Copy).then_inc(mesh_t_ok, 1)

        for u in range(2):
            mesh_copy(u, u, True)
        with act.Fori(1, NB // 2) as i:
            for u in range(2):
                mesh_copy(2 * i + u, u, False)
        act.wait_ge(tables_ok, 1)
        for c in range(NB):
            if c < NB - 1:
                act.wait_ge(count_mm, act.value_load(k["bucket_end"][0:1, c:c + 1], min_val=1, max_val=TILES))
            else:
                act.wait_ge(count_mm, TILES)
            for b in range(3):
                lo, hi = b * 512, min((b + 1) * 512, NB * P)
                act.activation(k["adj"][:, c, lo:hi], bank[b][:, 0:hi - lo], ACT.Copy)
            act.activation(k["degree"][:, c:c + 1], bank[3][:, 0:1], ACT.Copy).then_inc(counts_copied, 1)
            if c < NB - 1:
                act.wait_ge(counts_copied, c + 1)
                for b in range(3):
                    act.activation(bank[b][:], zeros16[:], ACT.Copy)
                act.activation(bank[3][:, 0:2], zeros16[:, 0:2], ACT.Copy).then_inc(wiped, 1)

    @block.tensor
    def _(pe):
        pe.wait_ge(dve_const, 4)
        pe.wait_ge(pool_const, 6)
        pe.wait_ge(totals_ok, 1)
        pe.matmul(bank[0][0:EP, 0:NB], before[0:EP, 0:EP], totals[:], start=True, stop=True)
        pe.matmul(bank[1][:, 0:NB], ones[0:EP, :], totals[:], start=True, stop=True).then_inc(totals_mm, 1)
        pe.wait_ge(centred, 3)
        pe.matmul(bank[2][:, 0:2], ones[:], bsum[:], start=True, stop=True).then_inc(bias_mm, 1)
        for i in range(2):
            for o in range(KC):
                if i:
                    pe.wait_ge(turned_out, o + 1)
                for c in range(KC):
                    last = pe.transpose(bank[4 + o][:, c * P:(c + 1) * P], w1[i][:, c, o * P:(o + 1) * P], k["ident"][:])
                last.then_inc(turned, 1)
        pe.wait_ge(cols_ok, 1)
        for i in range(2):
            for c in range(KC):
                last = pe.matmul(bank[3][:, i:i + 1], ones[:], cols[i][:, 3, c:c + 1], start=(c == 0), stop=(c == KC - 1),
                                 skip_group_check=True)
        last.then_inc(square_mm, 1)
        pe.wait_ge(gains_ok, 2)
        for j in range(NJ):
            _, left, right = matrices[j // KC]
            i = j % KC
            if j >= 2:
                pe.wait_ge(job_out_ok, j - 1)
            for c in range(KC):
                last = pe.matmul(bank[j % 2][:], left[:, c, i * P:(i + 1) * P], right[:, c, :],
                                 start=(c == 0), stop=(c == KC - 1))
            last.then_inc(job_mm, 1)
        for r in range(len(vectors)):
            _, left, right = vectors[r]
            if r < 2:
                pe.wait_ge(job_out_ok, NJ - 1 + r)
            else:
                pe.wait_ge(row_out_ok, r - 1)
            for c in range(KC):
                last = pe.matmul(bank[r % 2][0:1, :], left[:, c:c + 1], right[:, c, :], start=(c == 0), stop=(c == KC - 1))
            last.then_inc(job_mm, 1)
        def turn(n, u, fixed):
            pe.wait_ge(mesh_in[u], 16 if fixed else (n - u) * 8 + 16)
            if not fixed:
                pe.wait_ge(mesh_t_ok, n - 1)
            for c in range(KC):
                last = pe.transpose(bank[4 + u][:, c * P:c * P + NPB], mesh[u][:, c * P:(c + 1) * P], k["ident"][0:NPB, 0:NPB])
            last.then_inc(mesh_turned, 1)

        def multiply(n, u, fixed):
            pe.wait_ge(mesh_t_ok, n + 1)
            if not fixed:
                pe.wait_ge(mesh_ok, n - 1)
            for c in range(KC):
                last = pe.matmul(bank[6 + u][0:NPB, :], mesh_t[u][:, c, 0:NPB], w0b[:, c, :], start=(c == 0), stop=(c == KC - 1))
            last.then_inc(mesh_mm, 1)

        pe.wait_ge(turned_out, 2 * KC)
        for u in range(2):
            turn(u, u, True)
        for u in range(2):
            multiply(u, u, True)
        with pe.Fori(1, NB // 2) as i:
            for u in range(2):
                turn(2 * i + u, u, False)
            for u in range(2):
                multiply(2 * i + u, u, False)
        pe.wait_ge(dve_const, 7)
        pe.wait_ge(row_out_ok, len(vectors))
        pe.wait_ge(tables_ok, 1)
        for b in range(4):
            pe.matmul(bank[b][:], zeros16[:, 0:P], zeros16[:], start=True, stop=False, skip_group_check=True)

        def count(n, u, fixed):
            pe.wait_ge(hot_ok, n + 1)
            pe.wait_ge(wiped, pe.value_load(bucket_no[:, n:n + 1] if fixed else bucket_no[:, ds(n, 1)],
                                            min_val=1, max_val=NB))
            for s in range(NB):
                pe.matmul(bank[s // 4][:, (s % 4) * P:(s % 4 + 1) * P], hot_src[u][:, s * P:(s + 1) * P], hot_dst[u][:],
                          start=False, stop=False, skip_group_check=True)
            pe.matmul(bank[3][:, 0:2], hot_dst[u][:], ones16[:], start=False, stop=False,
                      skip_group_check=True).then_inc(count_mm, 1)

        bucket_no = k["tile_bucket1"][0:1, :]
        pe.sem_inc(wiped, 1)
        for u in range(2):
            count(u, u, True)
        with pe.Fori(1, TILES // 2) as i:
            for u in range(2):
                count(2 * i + u, u, False)


def need(engine, sem, value):
    if not isinstance(value, int) or value > 0:
        engine.wait_ge(sem, value)


def pairs(engine, body):
    body(0)
    with engine.Fori(1, NB // 2 - 1) as i:
        body(i)
    body(NB // 2 - 1)


def tile_of(tensor, n):
    return tensor[:, n, :] if isinstance(n, int) else tensor[:, ds(n, 1), :].rearrange("p a b -> p (a b)")


def node_rows(matrix, n):
    return matrix[n * NPB:(n + 1) * NPB, :] if isinstance(n, int) else matrix[ds(n * NPB, NPB), :]


LAYERS = 3


def phase_b(nc, ctx, t, scratch, keep):
    def sb(name, shape, dt=F32):
        return ctx.enter_context(nc.sbuf_tensor("b_" + name, shape, dt))

    def sem(name):
        return ctx.enter_context(nc.semaphore("b_" + name))

    bank = [ctx.enter_context(nc.psum_tensor(f"b_bank{i}", [P, 512], F32)) for i in range(8)]
    turn_bank, self_bank, neigh_bank, sum_bank = bank[0:2], bank[2:4], bank[4:6], bank[6:8]
    h = sb("h", [NPB, NB, D])
    u_hi, u_lo = sb("u_hi", [NPB, NB, D], F32R), sb("u_lo", [NPB, NB, D], F32R)
    w = [sb(f"w{i}", [P, KC, D]) for i in range(2)]
    w_hi = [sb(f"w_hi{i}", [P, KC, D], F32R) for i in range(2)]
    w_lo = [sb(f"w_lo{i}", [P, KC, D], F32R) for i in range(2)]
    bias = [sb(f"bias{i}", [NPB, D]) for i in range(2)]
    bias2 = sb("bias2", [NPB, D])
    hc = [sb(f"hc{i}", [NPB, D]) for i in range(2)]
    ht_hi = [sb(f"ht_hi{i}", [P, KC, P], F32R) for i in range(2)]
    ht_lo = [sb(f"ht_lo{i}", [P, KC, P], F32R) for i in range(2)]
    a_hi = [sb(f"a_hi{i}", [NPB, NB * P], F32R) for i in range(2)]
    a_lo = [sb(f"a_lo{i}", [NPB, NB * P], F32R) for i in range(2)]
    inv_degree = sb("inv_degree", [NPB, NB])
    mixed = [sb(f"mixed{i}", [NPB, D]) for i in range(2)]
    x = [sb(f"x{i}", [NPB, D]) for i in range(2)]
    out = [sb(f"out{i}", [NPB, 2, D]) for i in range(2)]
    stats = [sb(f"stats{i}", [NPB, 6]) for i in range(2)]
    moments = [sb(f"moments{i}", [NPB, 2]) for i in range(2)]
    dev = [sb(f"dev{i}", [NPB, 2]) for i in range(2)]
    k = keep

    h_in, w_in, bias_in = sem("h_in"), sem("w_in"), sem("bias_in")
    w_split, split_step, bias_free, chain_sem = sem("w_split"), sem("split_step"), sem("bias_free"), sem("chain")
    degree_ok, hc_ok, turned, ht_hi_ok, ht_lo_ok, prod_mm = (
        sem(n) for n in ("degree_ok", "hc_ok", "turned", "ht_hi_ok", "ht_lo_ok", "prod_mm"))
    self_ok, u_hi_ok, u_lo_ok = sem("self_ok"), sem("u_hi_ok"), sem("u_lo_ok")
    a_hi_ok, a_lo_ok, sum_mm, mixed_ok, h_ok = (sem(n) for n in ("a_hi_ok", "a_lo_ok", "sum_mm", "mixed_ok", "h_ok"))
    x_in = [sem(f"x_in{i}") for i in range(2)]
    res_ok, stats_ok, moments_ok, var_ok, dev_ok = (sem(n) for n in ("res_ok", "stats_ok", "moments_ok", "var_ok", "dev_ok"))
    out_ok = sem("out_ok")
    tick = sem("tick")
    x1_stored = [sem(f"x1_stored{i}") for i in range(2)]
    stored = [sem(f"stored{i}") for i in range(2)]

    weights = [(t["L0_gnn_Ws_self"][q], t["L0_gnn_Ws_neigh"][q]) for q in range(LAYERS)]
    weights.append((t["L1_gnn_node_W0"][0:D, :], t["L1_gnn_edge_W0"][2 * D:3 * D, :]))
    PASSES = LAYERS + 1

    def column(tensor, n):
        return tensor[:, n:n + 1] if isinstance(n, int) else tensor[:, ds(n, 1)]

    def spread(b):
        return b[:].rearrange("p (k n) -> p k n", k=KC)[:, :, 0:NPB]

    block = ctx.enter_context(nc.Block())

    @block.sync
    def _(sp):
        sp.dma_start(h[:], t["x"].rearrange("(b p) d -> p b d", p=NPB)).then_inc(h_in, 16)
        for q in range(PASSES):
            if q:
                sp.wait_ge(w_split, q)
            for i in range(2):
                sp.dma_start(w[i][:], chunked(weights[q][i])).then_inc(w_in, 16)
            if q < LAYERS:
                if q:
                    sp.wait_ge(self_ok, NB * q)
                sp.dma_start(bias[0][:], rows(t["L0_gnn_bs"][q]).broadcast_to([NPB, D])).then_inc(bias_in, 16)
        sp.wait_ge(self_ok, NB * LAYERS)
        sp.dma_start(bias[0][:], rows(t["L1_gnn_node_b0"]).broadcast_to([NPB, D])).then_inc(bias_in, 16)
        sp.dma_start(bias[1][:], rows(t["L1_gnn_edge_b0"]).broadcast_to([NPB, D])).then_inc(bias_in, 16)
        sp.dma_start(bias2[:], rows(scratch["edge_shift"]).broadcast_to([NPB, D])).then_inc(bias_in, 16)
        def residual(i):
            for u in range(2):
                n = 2 * i + u
                need(sp, res_ok, n - 1)
                sp.dma_start(x[u][:], node_rows(t["x"], n)).then_inc(x_in[u], 16)
            for u in range(2):
                n = 2 * i + u
                sp.wait_ge(out_ok, n + 1)
                sp.dma_start(node_rows(scratch["x1"], n), out[u][:, 0, :]).then_inc(x1_stored[u], 16)

        pairs(sp, residual)
        def results(i):
            for u in range(2):
                n = 2 * i + u
                sp.wait_ge(u_lo_ok, NB * LAYERS + n + 1)
                sp.dma_start(node_rows(scratch["node_own"], n), out[u][:, 0, :]).then_inc(stored[u], 16)
                sp.dma_start(node_rows(scratch["dst_table"], n), out[u][:, 1, :]).then_inc(stored[u], 16)

        pairs(sp, results)
        for u in range(2):
            sp.wait_ge(x1_stored[u], 16 * NB // 2)
            sp.wait_ge(stored[u], 32 * NB // 2)

    @block.gpsimd
    def _(pool):
        for q in range(PASSES):
            pool.wait_ge(w_in, 32 * (q + 1))
            need(pool, prod_mm, NB * q)
            for i in range(2):
                pool.tensor_copy(w_hi[i][:], w[i][:]).then_inc(split_step, 1)
            pool.wait_ge(split_step, 2 * (q + 1))
            pool.tensor_tensor(w_lo[0][:], w[0][:], w_hi[0][:].bitcast(F32), ALU.subtract)
            pool.tensor_tensor(w_lo[1][:], w[1][:], w_hi[1][:].bitcast(F32), ALU.subtract).then_inc(w_split, 1)

        def deviation(i):
            for u in range(2):
                n = 2 * i + u
                pool.wait_ge(var_ok, n + 1)
                pool.sem_inc(tick, 1)
                pool.tensor_tensor(dev[u][:, 1:2], dev[u][:, 0:1], k["half"][0:NPB, :], ALU.pow).then_inc(dev_ok, 1)

        pairs(pool, deviation)

    @block.vector
    def _(dve):
        chain = Chain(dve, chain_sem)
        chain.after(dve.tensor_scalar(inv_degree[:], k["degree"][0:NPB, :], 1.0, None, ALU.max))
        chain.after(dve.reciprocal(inv_degree[:], inv_degree[:]))

        def low(g, u):
            dve.wait_ge(ht_hi_ok, g + 1)
            need(dve, prod_mm, g - 1)
            dve.tensor_tensor(ht_lo[u][:, :, 0:NPB], spread(turn_bank[u]), ht_hi[u][:, :, 0:NPB].bitcast(F32),
                              ALU.subtract).then_inc(ht_lo_ok, 1)

        for q in range(PASSES):
            def evacuate(i, q=q):
                for u in range(2):
                    n = 2 * i + u
                    g = NB * q + n
                    if not (isinstance(n, int) and n == NB - 1):
                        low(g + 1, 1 - u)
                    dve.wait_ge(prod_mm, g + 1)
                    if q < LAYERS:
                        dve.tensor_tensor(tile_of(h, n), self_bank[u][0:NPB, :], bias[0][:], ALU.add).then_inc(self_ok, 1)
                        dve.wait_ge(u_hi_ok, g + 1)
                        dve.tensor_tensor(tile_of(u_lo, n), neigh_bank[u][0:NPB, :], tile_of(u_hi, n).bitcast(F32),
                                          ALU.subtract).then_inc(u_lo_ok, 1)
                    else:
                        if isinstance(n, int) and n < 2:
                            dve.wait_ge(x1_stored[u], 16 * NB // 2)
                        else:
                            dve.wait_ge(stored[u], (n - u) * 16)
                        dve.tensor_tensor(out[u][:, 0, :], self_bank[u][0:NPB, :], bias[0][:], ALU.add)
                        dve.tensor_tensor(out[u][:, 1, :], neigh_bank[u][0:NPB, :], bias[1][:], ALU.add).then_inc(u_lo_ok, 1)

            dve.wait_ge(bias_in, 16 * (q + 1) if q < LAYERS else 16 * (q + 3))
            if q == LAYERS:
                chain.after(dve.tensor_tensor(bias[1][:], bias[1][:], bias2[:], ALU.add))
            low(NB * q, 0)
            pairs(dve, evacuate)
            if q == LAYERS:
                break

            def mix(i, q=q):
                for u in range(2):
                    n = 2 * i + u
                    g = NB * q + n
                    dve.wait_ge(a_hi_ok, g + 1)
                    need(dve, sum_mm, g - 1)
                    dve.tensor_tensor(a_lo[u][:], tile_of(k["adj"], n)[0:NPB, :], a_hi[u][:].bitcast(F32),
                                      ALU.subtract).then_inc(a_lo_ok, 1)
                for u in range(2):
                    n = 2 * i + u
                    g = NB * q + n
                    dve.wait_ge(sum_mm, g + 1)
                    if q < LAYERS - 1:
                        need(dve, h_ok, g - 1)
                    dve.scalar_tensor_tensor(out=mixed[u][:], in0=sum_bank[u][0:NPB, :], scalar=column(inv_degree, n),
                                             in1=tile_of(h, n), op0=ALU.mult, op1=ALU.add).then_inc(mixed_ok, 1)
                if q < LAYERS - 1:
                    return
                for u in range(2):
                    n = 2 * i + u
                    dve.wait_ge(x_in[u], (n - u) * 8 + 16)
                    dve.wait_ge(mixed_ok, NB * q + n + 1)
                    dve.tensor_tensor(mixed[u][:], mixed[u][:], x[u][:], ALU.add).then_inc(res_ok, 1)
                for u in range(2):
                    dve.wait_ge(res_ok, 2 * i + u + 1)
                    dve.bn_stats(stats[u][:], mixed[u][:]).then_inc(stats_ok, 1)
                for u in range(2):
                    dve.wait_ge(stats_ok, 2 * i + u + 1)
                    dve.sem_inc(tick, 1)
                    dve.bn_aggr(moments[u][:], stats[u][:]).then_inc(moments_ok, 1)
                for u in range(2):
                    dve.wait_ge(moments_ok, 2 * i + u + 1)
                    dve.tensor_scalar(dev[u][:, 0:1], moments[u][:, 1:2], EPS, None, ALU.add).then_inc(var_ok, 1)
                for u in range(2):
                    n = 2 * i + u
                    dve.wait_ge(dev_ok, n + 1)
                    if not (isinstance(n, int) and n < 2):
                        dve.wait_ge(x1_stored[u], (n - u) * 8)
                    dve.tensor_scalar(tile_of(h, n), mixed[u][:], moments[u][:, 0:1], dev[u][:, 1:2],
                                      ALU.subtract, ALU.mult).then_inc(h_ok, 1)
                    dve.tensor_scalar(out[u][:, 0, :], mixed[u][:], moments[u][:, 0:1], dev[u][:, 1:2],
                                      ALU.subtract, ALU.mult).then_inc(out_ok, 1)

            pairs(dve, mix)

    @block.scalar
    def _(act):
        def copy_h(q, n, u):
            g = NB * q + n
            if q:
                act.wait_ge(h_ok, NB * (q - 1) + n + 1)
            need(act, turned, g - 1)
            act.activation(hc[u][:], tile_of(h, n), ACT.Copy).then_inc(hc_ok, 1)

        def high(g, u):
            act.wait_ge(turned, g + 1)
            need(act, prod_mm, g - 1)
            act.activation(ht_hi[u][:, :, 0:NPB], spread(turn_bank[u]), ACT.Copy).then_inc(ht_hi_ok, 1)

        act.wait_ge(h_in, 16)
        for q in range(PASSES):
            def evacuate(i, q=q):
                for u in range(2):
                    n = 2 * i + u
                    g = NB * q + n
                    if not (isinstance(n, int) and n == NB - 1):
                        copy_h(q, n + 1, 1 - u)
                        high(g + 1, 1 - u)
                    if q < LAYERS:
                        act.wait_ge(prod_mm, g + 1)
                        act.activation(tile_of(u_hi, n), neigh_bank[u][0:NPB, :], ACT.Copy).then_inc(u_hi_ok, 1)

            copy_h(q, 0, 0)
            high(NB * q, 0)
            pairs(act, evacuate)
            if q == LAYERS:
                break

            def rectify(i, q=q):
                for u in range(2):
                    n = 2 * i + u
                    g = NB * q + n
                    need(act, sum_mm, g - 1)
                    act.activation(a_hi[u][:], tile_of(k["adj"], n)[0:NPB, :], ACT.Copy).then_inc(a_hi_ok, 1)
                if q < LAYERS - 1:
                    for u in range(2):
                        n = 2 * i + u
                        act.wait_ge(mixed_ok, NB * q + n + 1)
                        act.activation(tile_of(h, n), mixed[u][:], ACT.Relu).then_inc(h_ok, 1)

            pairs(act, rectify)

    @block.tensor
    def _(pe):
        def turn(g, u):
            pe.wait_ge(hc_ok, g + 1)
            need(pe, ht_lo_ok, g - 1)
            for c in range(KC):
                last = pe.transpose(turn_bank[u][:, c * P:c * P + NPB], hc[u][:, c * P:(c + 1) * P], k["ident"][0:NPB, 0:NPB])
            last.then_inc(turned, 1)

        for q in range(PASSES):
            def multiply(i, q=q):
                for u in range(2):
                    n = 2 * i + u
                    g = NB * q + n
                    if not (isinstance(n, int) and n == NB - 1):
                        turn(g + 1, 1 - u)
                    pe.wait_ge(ht_lo_ok, g + 1)
                    if q < LAYERS:
                        need(pe, self_ok, g - 1)
                    need(pe, u_lo_ok, g - 1)
                    left = (lambda c: ht_hi[u][:, c, 0:NPB], lambda c: ht_lo[u][:, c, 0:NPB])
                    for b, j in ((self_bank, 0), (neigh_bank, 1)):
                        last = product(pe, b[u][0:NPB, :], left, (lambda c: w_hi[j][:, c, :], lambda c: w_lo[j][:, c, :]), range(KC))
                    last.then_inc(prod_mm, 1)

            turn(NB * q, 0)
            pe.wait_ge(w_split, q + 1)
            pairs(pe, multiply)
            if q == LAYERS:
                break
            pe.wait_ge(u_lo_ok, NB * (q + 1))

            def add_up(i, q=q):
                for u in range(2):
                    g = NB * q + 2 * i + u
                    pe.wait_ge(a_lo_ok, g + 1)
                    need(pe, mixed_ok, g - 1)
                    last = product(pe, sum_bank[u][:], (lambda s: a_hi[u][:, s * P:(s + 1) * P], lambda s: a_lo[u][:, s * P:(s + 1) * P]),
                                   (lambda s: u_hi[:, s, :], lambda s: u_lo[:, s, :]), range(NB))
                    last.then_inc(sum_mm, 1)

            pairs(pe, add_up)


def phase_c(nc, ctx, t, scratch, keep):
    def sb(name, shape, dt=F32):
        return ctx.enter_context(nc.sbuf_tensor("c_" + name, shape, dt))

    def sem(name):
        return ctx.enter_context(nc.semaphore("c_" + name))

    def psum(name, width=512):
        return ctx.enter_context(nc.psum_tensor("c_" + name, [P, 512], F32))

    feat_bank, var1_bank, edge_bank, turn_bank, var2_bank = (
        psum(n) for n in ("feat_bank", "var1_bank", "edge_bank", "turn_bank", "var2_bank"))
    sum_p_bank, sum_h_bank, sum_r_bank = psum("sum_p_bank"), psum("sum_h_bank"), psum("sum_r_bank")
    mats = ("square1", "fold_edge", "square2")
    biases = ("lin1", "fold_edge_b", "lin2")
    m_hi = [sb(f"m_hi{i}", [P, KC, D], F32R) for i in range(3)]
    m_lo = [sb(f"m_lo{i}", [P, KC, D], F32R) for i in range(3)]
    bias = sb("bias", [P, 3, D])
    w0 = sb("w0", [P, D], F32R)
    zeros16 = sb("zeros16", [P, 512], BF16)
    attr_hi = sb("attr_hi", [P, GROUP, A4], F32R)
    stack = sb("stack", [P, GROUP, STK])
    attr_t = sb("attr_t", [P, P], F32R)
    at_nodes = [sb(f"at_nodes{i}", [P, 2], I32) for i in range(4)]
    node_at = sb("node_at", [P, TILES, 2], I32)
    dst_in = sb("dst_in", [P, TILES])
    from_src = [sb(f"from_src{i}", [P, D]) for i in range(4)]
    from_dst = [sb(f"from_dst{i}", [P, D]) for i in range(4)]
    pt_f = [sb(f"pt_f{i}", [P, KC, P]) for i in range(2)]
    pt_hi = [sb(f"pt_hi{i}", [P, KC, P], F32R) for i in range(2)]
    pt_lo = [sb(f"pt_lo{i}", [P, KC, P], F32R) for i in range(2)]
    p = [sb(f"p{i}", [P, D]) for i in range(2)]
    h = [sb(f"h{i}", [P, D]) for i in range(2)]
    ht_hi = [sb(f"ht_hi{i}", [P, KC, P], F32R) for i in range(2)]
    ht_lo = [sb(f"ht_lo{i}", [P, KC, P], F32R) for i in range(2)]
    hot = [sb(f"hot{i}", [P, P], F32R) for i in range(4)]
    var = [sb(f"var{i}", [P, 4]) for i in range(4)]
    dev = [sb(f"dev{i}", [P, 4]) for i in range(4)]
    with ExitStack() as early:
        def sb_early(name, shape, dt=F32):
            return early.enter_context(nc.sbuf_tensor("c_" + name, shape, dt))

        staging = sb_early("staging", [P, KC, D])
        w0_f, w0_hi, w0_lo = sb_early("w0_f", [A4 + 1, D]), sb_early("w0_hi", [A4 + 1, D], F32R), sb_early("w0_lo", [A4 + 1, D], F32R)
    rp_hi = [sb(f"rp_hi{i}", [P, D], F32R) for i in range(4)]
    rp_lo = [sb(f"rp_lo{i}", [P, D], F32R) for i in range(4)]
    rh_hi = [sb(f"rh_hi{i}", [P, D], F32R) for i in range(2)]
    rh_lo = [sb(f"rh_lo{i}", [P, D], F32R) for i in range(2)]
    k = keep

    mat_in, small_in, split_ok, mat_hi_ok = sem("mat_in"), sem("small_in"), sem("split_ok"), sem("mat_hi_ok")
    opened = sem("opened")
    rows_split, placed, set_up, tick, w0_zero = sem("rows_split"), sem("placed"), sem("set_up"), sem("tick"), sem("w0_zero")
    attr_hi_ok, stack_ok, stack_turned, attr_t_ok = (sem(n) for n in ("attr_hi_ok", "stack_ok", "stack_turned", "attr_t_ok"))
    pt_mm, p_mm, pt_hi_ok, pt_f_ok, p_ok, pt_lo_ok = (sem(n) for n in ("pt_mm", "p_mm", "pt_hi_ok", "pt_f_ok", "p_ok", "pt_lo_ok"))
    var1_mm, var1_ok, bound1_ok, dev1_ok = (sem(n) for n in ("var1_mm", "var1_ok", "bound1_ok", "dev1_ok"))
    at_ok, added_ok, edge_mm, z_ok, h_ok = (sem(n) for n in ("at_ok", "added_ok", "edge_mm", "z_ok", "h_ok"))
    bias_in = sem("bias_in")
    var1_set, edge_set, var2_set = sem("var1_set"), sem("edge_set"), sem("var2_set")
    src_in = [sem(f"src_in{i}") for i in range(4)]
    dst_rows_in = [sem(f"dst_in{i}") for i in range(4)]
    h_turned, ht_hi_ok, ht_lo_ok = sem("h_turned"), sem("ht_hi_ok"), sem("ht_lo_ok")
    var2_mm, var2_ok, bound2_ok, dev2_ok = (sem(n) for n in ("var2_mm", "var2_ok", "bound2_ok", "dev2_ok"))
    rp_hi_ok, rp_lo_ok, rh_hi_ok, rh_lo_ok, hot_ok = (sem(n) for n in ("rp_hi_ok", "rp_lo_ok", "rh_hi_ok", "rh_lo_ok", "hot_ok"))
    sums_mm, sums_read, sums_left = sem("sums_mm"), sem("sums_read"), sem("sums_left")

    def steps(engine, step):
        for u in range(GROUP):
            step(0, u)
        with engine.Fori(1, GROUPS - 1) as i:
            for u in range(GROUP):
                step(i, u)
        for u in range(GROUP):
            step(GROUPS - 1, u)

    def at(tensor, n, width=1):
        return tensor[:, n:n + width] if isinstance(n, int) else tensor[:, ds(n, width)]

    def exists(n):
        return not isinstance(n, int) or 0 <= n < TILES

    block = ctx.enter_context(nc.Block())

    @block.sync
    def _(sp):
        sp.dma_start(w0_f[0:A4, :], t["L1_gnn_emb_W0"]).then_inc(small_in, 16)
        sp.dma_start(w0_f[A4:A4 + 1, :], rows(t["L1_gnn_emb_b0"])).then_inc(small_in, 16)
        for i, name in enumerate(biases):
            sp.dma_start(bias[:, i, :], rows(scratch[name]).broadcast_to([P, D])).then_inc(bias_in, 16)
        sp.dma_start(staging[:], chunked(scratch[mats[0]])).then_inc(mat_in, 16)
        sp.wait_ge(rows_split, 2)
        sp.wait_ge(w0_zero, 1)
        for j in range(GROUP):
            base = STK * j
            sp.dma_start(w0[base:base + 5, :].bitcast(F32), w0_hi[:].bitcast(F32)).then_inc(placed, 16)
            sp.dma_start(w0[base + 5:base + 10, :].bitcast(F32), w0_lo[:].bitcast(F32)).then_inc(placed, 16)
            sp.dma_start(w0[base + 10:base + 14, :].bitcast(F32), w0_hi[0:A4, :].bitcast(F32)).then_inc(placed, 16)
        for i in (1, 2):
            sp.wait_ge(split_ok, i)
            sp.dma_start(staging[:], chunked(scratch[mats[i]])).then_inc(mat_in, 16)

    @block.gpsimd
    def _(pool):
        def build_stack(g):
            rec = k["recs"][:, g * GROUP:(g + 1) * GROUP, :] if isinstance(g, int) else k["recs"][:, ds(g * GROUP, GROUP), :]
            attr = rec[:, :, F_ATTR:F_ATTR + A4]
            if not isinstance(g, int) or g:
                pool.wait_ge(stack_turned, g)
                pool.sem_inc(tick, 1)
            pool.tensor_copy(attr_hi[:], attr).then_inc(attr_hi_ok, 1)
            pool.wait_ge(attr_hi_ok, g + 1)
            pool.sem_inc(tick, 1)
            pool.tensor_copy(stack[:, :, 0:A4], attr_hi[:].bitcast(F32))
            pool.tensor_copy(stack[:, :, 5:5 + A4], attr_hi[:].bitcast(F32))
            pool.tensor_tensor(stack[:, :, 10:10 + A4], attr, attr_hi[:].bitcast(F32), ALU.subtract).then_inc(stack_ok, 1)

        def gather(n, u):
            if not isinstance(n, int) or n >= 4:
                pool.wait_ge(h_ok, n - 3)
                pool.sem_inc(tick, 1)
            pool.tensor_copy(at_nodes[u][:], node_at[:, n, :] if isinstance(n, int)
                             else node_at[:, ds(n, 1), :].rearrange("p a b -> p (a b)")).then_inc(at_ok, 1)
            pool.wait_ge(at_ok, n + 1)
            pool.sem_inc(tick, 1)
            pool.indirect_dma_start(from_src[u][:], None, scratch["mesh_table"],
                                    bass.IndirectOffsetOnAxis(ap=at_nodes[u][:, 0:1], axis=0)).then_inc(src_in[u], 16)
            pool.indirect_dma_start(from_dst[u][:], None, scratch["dst_table"],
                                    bass.IndirectOffsetOnAxis(ap=at_nodes[u][:, 1:2], axis=0)).then_inc(dst_rows_in[u], 16)

        def add(n, u):
            pool.wait_ge(src_in[u], (n - u) * 4 + 16)
            pool.wait_ge(dst_rows_in[u], (n - u) * 4 + 16)
            pool.sem_inc(tick, 1)
            pool.tensor_tensor(from_src[u][:], from_src[u][:], from_dst[u][:], ALU.add).then_inc(added_ok, 1)

        def step(i, u):
            n = GROUP * i + u
            if exists(n + 3):
                gather(n + 3, (u + 3) % 4)
            if u == 0 and exists(n + GROUP):
                build_stack(i + 1)
            pool.wait_ge(bound1_ok, n + 1)
            pool.tensor_tensor(dev[u][:, 0:1], var[u][:, 2:3], k["half"][:], ALU.pow).then_inc(dev1_ok, 1)
            if exists(n + 1):
                add(n + 1, (u + 1) % 4)
            if exists(n - 1):
                v = (u - 1) % 4
                pool.wait_ge(bound2_ok, n)
                pool.tensor_tensor(dev[v][:, 1:2], var[v][:, 3:4], k["half"][:], ALU.pow).then_inc(dev2_ok, 1)

        pool.wait_ge(set_up, 1)
        for u in range(3):
            gather(u, u)
        build_stack(0)
        add(0, 0)
        steps(pool, step)
        pool.wait_ge(bound2_ok, TILES)
        pool.tensor_tensor(dev[3][:, 1:2], var[3][:, 3:4], k["half"][:], ALU.pow).then_inc(dev2_ok, 1)

    @block.vector
    def _(dve):
        dve.memset(stack[:], 0.0)
        dve.tensor_copy(node_at[:, :, 0], k["recs"][:, :, F_SRC])
        dve.tensor_copy(node_at[:, :, 1], k["recs"][:, :, F_DSTG])
        dve.tensor_copy(dst_in[:], k["recs"][:, :, F_DST])
        for u in range(4):
            dve.memset(dev[u][:, 2:3], 1.0)
            dve.memset(dev[u][:, 3:4], 0.0)
        dve.memset(zeros16[:], 0.0)
        dve.memset(w0[:].bitcast(F32), 0.0).then_inc(w0_zero, 1)
        dve.wait_ge(w0_zero, 1)
        dve.memset(stack[:, :, A4:A4 + 1], 1.0)
        dve.memset(stack[:, :, 2 * A4 + 1:2 * A4 + 2], 1.0).then_inc(set_up, 1)
        dve.wait_ge(rows_split, 1)
        dve.tensor_tensor(w0_lo[:], w0_f[:], w0_hi[:].bitcast(F32), ALU.subtract).then_inc(rows_split, 1)
        for i in range(3):
            dve.wait_ge(mat_hi_ok, i + 1)
            dve.tensor_tensor(m_lo[i][:], staging[:], m_hi[i][:].bitcast(F32), ALU.subtract).then_inc(split_ok, 1)

        def low_p(n, u):
            dve.wait_ge(pt_f_ok, n + 1)
            need(dve, edge_mm, n - 1)
            dve.tensor_tensor(pt_lo[u % 2][:], pt_f[u % 2][:], pt_hi[u % 2][:].bitcast(F32), ALU.subtract).then_inc(pt_lo_ok, 1)

        def low_rh(n, u):
            dve.wait_ge(rh_hi_ok, n + 1)
            need(dve, sums_mm, n - 1)
            dve.scalar_tensor_tensor(out=rh_lo[u % 2][:], in0=h[u % 2][:], scalar=dev[u][:, 1:2], in1=rh_hi[u % 2][:].bitcast(F32),
                                     op0=ALU.mult, op1=ALU.subtract).then_inc(rh_lo_ok, 1)
            dve.tensor_scalar(hot[u][:], k["grid"][:], at(dst_in, n), None, ALU.is_equal).then_inc(hot_ok, 1)

        def leave(n):
            last = dve.value_load(at(k["tile_last"][0:1, :], n), min_val=0, max_val=NB)
            with dve.If(last > 0):
                b = nc.s_assert_within(last - 1, 0, NB - 1)
                dve.wait_ge(sums_mm, n + 1)
                dve.sem_inc(tick, 1)
                dve.tensor_copy(tile_of(k["sum_p"], b), sum_p_bank[:])
                dve.tensor_copy(tile_of(k["sum_h"], b), sum_h_bank[:])
                dve.tensor_copy(tile_of(k["sum_r"], b), sum_r_bank[:, 0:4]).then_inc(sums_read, 1)
                dve.wait_ge(sums_read, last)
                dve.memset(sum_p_bank[:], 0.0)
                dve.memset(sum_h_bank[:], 0.0)
                dve.memset(sum_r_bank[:, 0:4], 0.0).then_inc(sums_left, 1)

        def variance2(n, u):
            dve.wait_ge(var2_mm, n + 1)
            dve.tensor_tensor_reduce(var2_bank[:], var2_bank[:], h[u % 2][:], 1.0 / D, k["floor"][:, 1:2],
                                     ALU.mult, ALU.add, var[u][:, 1:2]).then_inc(var2_ok, 1)
            dve.wait_ge(var2_ok, n + 1)
            dve.tensor_scalar(var[u][:, 3:4], var[u][:, 1:2], EPS, None, ALU.max).then_inc(bound2_ok, 1)

        def low_ht(n, u):
            dve.wait_ge(ht_hi_ok, n + 1)
            need(dve, var2_mm, n - 1)
            dve.tensor_tensor(ht_lo[u % 2][:], turn_bank[:].rearrange("p (k n) -> p k n", k=KC), ht_hi[u % 2][:].bitcast(F32),
                              ALU.subtract).then_inc(ht_lo_ok, 1)

        def step(i, u):
            n = GROUP * i + u
            if exists(n - 3):
                leave(n - 3)
            dve.wait_ge(var1_mm, n + 1)
            dve.wait_ge(p_ok, n + 1)
            dve.tensor_tensor_reduce(var1_bank[:], var1_bank[:], p[u % 2][:], 1.0 / D, k["floor"][:, 0:1],
                                     ALU.mult, ALU.add, var[u][:, 0:1]).then_inc(var1_ok, 1)
            dve.wait_ge(var1_ok, n + 1)
            dve.tensor_scalar(var[u][:, 2:3], var[u][:, 0:1], EPS, None, ALU.max).then_inc(bound1_ok, 1)
            if exists(n - 2):
                low_rh(n - 2, (u - 2) % 4)
            if exists(n + 1):
                low_p(n + 1, (u + 1) % 4)
            if exists(n - 1):
                low_ht(n - 1, (u - 1) % 4)
            dve.wait_ge(rp_hi_ok, n + 1)
            dve.scalar_tensor_tensor(out=rp_lo[u][:], in0=p[u % 2][:], scalar=dev[u][:, 0:1], in1=rp_hi[u][:].bitcast(F32),
                                     op0=ALU.mult, op1=ALU.subtract).then_inc(rp_lo_ok, 1)
            dve.wait_ge(edge_mm, n + 1)
            dve.wait_ge(added_ok, n + 1)
            dve.scalar_tensor_tensor(out=from_src[u][:], in0=edge_bank[:], scalar=dev[u][:, 0:1], in1=from_src[u][:],
                                     op0=ALU.mult, op1=ALU.add).then_inc(z_ok, 1)
            if exists(n - 1):
                variance2(n - 1, (u - 1) % 4)

        low_p(0, 0)
        steps(dve, step)
        last = TILES - 1
        low_ht(last, 3)
        leave(last - 2)
        low_rh(last - 1, 2)
        variance2(last, 3)
        leave(last - 1)
        low_rh(last, 3)
        leave(last)

    @block.scalar
    def _(act):
        act.wait_ge(small_in, 32)
        act.activation(w0_hi[:], w0_f[:], ACT.Copy).then_inc(rows_split, 1)
        for i in range(3):
            act.wait_ge(mat_in, 16 * (i + 1))
            act.activation(m_hi[i][:], staging[:], ACT.Copy).then_inc(mat_hi_ok, 1)

        def turn_out(g):
            act.wait_ge(stack_turned, g + 1)
            act.activation(attr_t[:], turn_bank[:, 0:P], ACT.Copy).then_inc(attr_t_ok, 1)

        def hidden(n, u):
            act.wait_ge(pt_mm, n + 1)
            need(act, pt_lo_ok, n - 1)
            need(act, edge_mm, n - 1)
            act.activation(pt_hi[u % 2][:], feat_bank[:].rearrange("p (k n) -> p k n", k=KC), ACT.Silu).then_inc(pt_hi_ok, 1)
            act.activation(pt_f[u % 2][:], feat_bank[:].rearrange("p (k n) -> p k n", k=KC), ACT.Silu).then_inc(pt_f_ok, 1)

        def hidden_rows(n, u):
            act.wait_ge(p_mm, n + 1)
            need(act, rp_lo_ok, n - 1)
            act.activation(p[u % 2][:], feat_bank[:], ACT.Silu).then_inc(p_ok, 1)

        def high_rh(n, u):
            act.wait_ge(dev2_ok, n + 1)
            need(act, sums_mm, n - 1)
            act.activation(rh_hi[u % 2][:], h[u % 2][:], ACT.Copy, scale=dev[u][:, 1:2]).then_inc(rh_hi_ok, 1)

        def high_ht(n, u):
            act.wait_ge(h_turned, n + 1)
            need(act, var2_mm, n - 1)
            act.activation(ht_hi[u % 2][:], turn_bank[:].rearrange("p (k n) -> p k n", k=KC), ACT.Copy).then_inc(ht_hi_ok, 1)

        def bias_into(bank, m, bank_set):
            act.activation(bank[:], bias[:, m, :], ACT.Copy).then_inc(bank_set, 1)

        def step(i, u):
            n = GROUP * i + u
            if u == GROUP - 1 and exists(n + 1):
                turn_out(i + 1)
            if exists(n + 1):
                hidden(n + 1, (u + 1) % 4)
            if exists(n - 1):
                need(act, var2_ok, n - 1)
                bias_into(var2_bank, 2, var2_set)
            if exists(n - 2):
                high_rh(n - 2, (u - 2) % 4)
            if exists(n + 1):
                hidden_rows(n + 1, (u + 1) % 4)
            if exists(n - 1):
                high_ht(n - 1, (u - 1) % 4)
            if exists(n + 1):
                act.wait_ge(var1_ok, n + 1)
                bias_into(var1_bank, 0, var1_set)
            act.wait_ge(dev1_ok, n + 1)
            need(act, sums_mm, n - 3)
            act.activation(rp_hi[u][:], p[u % 2][:], ACT.Copy, scale=dev[u][:, 0:1]).then_inc(rp_hi_ok, 1)
            act.wait_ge(z_ok, n + 1)
            need(act, rh_lo_ok, n - 1)
            need(act, h_turned, n - 1)
            act.activation(h[u % 2][:], from_src[u][:], ACT.Silu).then_inc(h_ok, 1)
            if exists(n + 1):
                bias_into(edge_bank, 1, edge_set)

        act.wait_ge(bias_in, 48)
        act.wait_ge(opened, 1)
        bias_into(var1_bank, 0, var1_set)
        bias_into(edge_bank, 1, edge_set)
        turn_out(0)
        hidden(0, 0)
        hidden_rows(0, 0)
        steps(act, step)
        last = TILES - 1
        act.wait_ge(var2_ok, last)
        bias_into(var2_bank, 2, var2_set)
        high_ht(last, 3)
        high_rh(last - 1, 2)
        high_rh(last, 3)

    @block.tensor
    def _(pe):
        def turn_stack(g):
            pe.wait_ge(stack_ok, g + 1)
            pe.transpose(turn_bank[:, 0:P], stack[:].rearrange("p t f -> p (t f)"), k["ident"][:]).then_inc(stack_turned, 1)

        def features(n, u):
            need(pe, p_ok, n)
            part = slice(STK * u, STK * (u + 1))
            for c in range(KC):
                last = pe.matmul(feat_bank[:, c * P:(c + 1) * P], w0[part, c * P:(c + 1) * P], attr_t[part, :],
                                 start=True, stop=True, skip_group_check=True)
            last.then_inc(pt_mm, 1)

        def feature_rows(n, u):
            pe.wait_ge(pt_f_ok, n + 1)
            part = slice(STK * u, STK * (u + 1))
            pe.matmul(feat_bank[:], attr_t[part, :], w0[part, :], start=True, stop=True).then_inc(p_mm, 1)

        def square(out, left, m):
            for c in range(KC):
                part = SQUARE_BLOCKS[c]
                to, high, low = (b.rearrange("p (k n) -> p k n", k=KC)[:, part, :] for b in (out[:], m_hi[m][:, c, :], m_lo[m][:, c, :]))
                pe.matmul(to, left[0][:, c, :], high, start=False, stop=False, skip_group_check=True)
                pe.matmul(to, left[0][:, c, :], low, start=False, stop=False, skip_group_check=True)
                last = pe.matmul(to, left[1][:, c, :], high, start=False, stop=(c == KC - 1), skip_group_check=True)
            return last

        def turn_h(n, u):
            pe.wait_ge(h_ok, n + 1)
            need(pe, ht_lo_ok, n)
            for c in range(KC):
                last = pe.transpose(turn_bank[:, c * P:(c + 1) * P], h[u % 2][:, c * P:(c + 1) * P], k["ident"][:])
            last.then_inc(h_turned, 1)

        def variance2(n, u):
            pe.wait_ge(ht_lo_ok, n + 1)
            pe.wait_ge(var2_set, n + 1)
            square(var2_bank, (ht_hi[u % 2], ht_lo[u % 2]), 2).then_inc(var2_mm, 1)

        def sums(n, u):
            pe.wait_ge(rp_lo_ok, n + 1)
            pe.wait_ge(hot_ok, n + 1)
            pe.wait_ge(sums_left, pe.value_load(at(k["tile_bucket1"][0:1, :], n), min_val=1, max_val=NB))
            for bank, part in ((sum_p_bank, rp_hi[u]), (sum_p_bank, rp_lo[u]), (sum_h_bank, rh_hi[u % 2]), (sum_h_bank, rh_lo[u % 2])):
                pe.matmul(bank[:], hot[u][:], part[:], start=False, stop=False, skip_group_check=True)
            pe.matmul(sum_r_bank[:, 0:4], hot[u][:].bitcast(F32), dev[u][:], start=False, stop=False,
                      skip_group_check=True).then_inc(sums_mm, 1)

        def step(i, u):
            n = GROUP * i + u
            if u == GROUP - 1 and exists(n + 1):
                pe.wait_ge(attr_t_ok, i + 2)
            if exists(n + 1):
                features(n + 1, (u + 1) % 4)
            pe.wait_ge(pt_lo_ok, n + 1)
            pe.wait_ge(var1_set, n + 1)
            square(var1_bank, (pt_hi[u % 2], pt_lo[u % 2]), 0).then_inc(var1_mm, 1)
            if exists(n + 1):
                feature_rows(n + 1, (u + 1) % 4)
            if exists(n - 1):
                turn_h(n - 1, (u - 1) % 4)
            pe.wait_ge(edge_set, n + 1)
            for c in range(KC):
                left = (pt_hi[u % 2][:, c, :], pt_lo[u % 2][:, c, :])
                pe.matmul(edge_bank[:], left[0], m_hi[1][:, c, :], start=False, stop=False, skip_group_check=True)
                pe.matmul(edge_bank[:], left[0], m_lo[1][:, c, :], start=False, stop=False, skip_group_check=True)
                last = pe.matmul(edge_bank[:], left[1], m_hi[1][:, c, :], start=False, stop=(c == KC - 1), skip_group_check=True)
            last.then_inc(edge_mm, 1)
            if exists(n - 1):
                variance2(n - 1, (u - 1) % 4)
            if u == GROUP - 2 and exists(n + 2):
                turn_stack(i + 1)
            if exists(n - 2):
                sums(n - 2, (u - 2) % 4)

        pe.wait_ge(set_up, 1)
        for bank in (sum_p_bank, sum_h_bank, sum_r_bank, var1_bank, edge_bank, var2_bank):
            last = pe.matmul(bank[:], zeros16[:, 0:P], zeros16[:], start=True, stop=False, skip_group_check=True)
        last.then_inc(opened, 1)
        pe.sem_inc(sums_left, 1)
        pe.wait_ge(placed, 16 * 3 * GROUP)
        turn_stack(0)
        pe.wait_ge(attr_t_ok, 1)
        features(0, 0)
        feature_rows(0, 0)
        pe.wait_ge(split_ok, 3)
        steps(pe, step)
        last = TILES - 1
        turn_h(last, 3)
        sums(last - 1, 2)
        variance2(last, 3)
        sums(last, 3)


def phase_d(nc, ctx, t, scratch, keep, out_dram):
    def sb(name, shape, dt=F32):
        return ctx.enter_context(nc.sbuf_tensor("d_" + name, shape, dt))

    def sem(name):
        return ctx.enter_context(nc.semaphore("d_" + name))

    def psum(name):
        return ctx.enter_context(nc.psum_tensor("d_" + name, [P, 512], F32))

    turn_bank = [psum(f"turn_bank{i}") for i in range(2)]
    small_bank, hidden_bank, hturn_bank, node_bank = (psum(n) for n in ("small_bank", "hidden_bank", "hturn_bank", "node_bank"))
    mats = (scratch["fold_node1"], scratch["fold_node2"], t["L1_gnn_node_W1"])
    m_f = [sb(f"m_f{i}", [P, KC, D]) for i in range(3)]
    m_hi = [sb(f"m_hi{i}", [P, KC, D], F32R) for i in range(3)]
    m_lo = [sb(f"m_lo{i}", [P, KC, D], F32R) for i in range(3)]
    row_fold = sb("row_fold", [4, D])
    b1, gain, shift = (sb(n, [NPB, D]) for n in ("b1", "gain", "shift"))
    s_in = [[sb(f"s_in{j}{i}", [NPB, D]) for i in range(2)] for j in range(2)]
    r_in = [sb(f"r_in{i}", [NPB, 4]) for i in range(2)]
    s_hi = [sb(f"s_hi{j}", [P, KC, P], F32R) for j in range(2)]
    s_lo = [sb(f"s_lo{j}", [P, KC, P], F32R) for j in range(2)]
    r_t = sb("r_t", [4, NPB])
    own = [sb(f"own{i}", [NPB, D]) for i in range(2)]
    x1 = [sb(f"x1{i}", [NPB, D]) for i in range(2)]
    hidden, y, final = sb("hidden", [NPB, D]), sb("y", [NPB, D]), [sb(f"final{i}", [NPB, D]) for i in range(2)]
    nt_hi, nt_lo = sb("nt_hi", [P, KC, P], F32R), sb("nt_lo", [P, KC, P], F32R)
    stats, moments, dev = (sb(n, [NPB, 8]) for n in ("stats", "moments", "dev"))
    k = keep

    mat_in, row_in, mat_ok, mat_hi_ok, tick, zeroed = (sem(n) for n in ("mat_in", "row_in", "mat_ok", "mat_hi_ok", "tick", "zeroed"))
    tile_in = [sem(f"tile_in{i}") for i in range(2)]
    stored = [sem(f"stored{i}") for i in range(2)]
    copied, turned, r_turned, s_hi_ok, s_lo_ok, r_t_ok = (
        sem(n) for n in ("copied", "turned", "r_turned", "s_hi_ok", "s_lo_ok", "r_t_ok"))
    hidden_mm, own_ok, hidden_ok, hidden_turned, nt_hi_ok, nt_lo_ok, node_mm = (
        sem(n) for n in ("hidden_mm", "own_ok", "hidden_ok", "hidden_turned", "nt_hi_ok", "nt_lo_ok", "node_mm"))
    y_step, var_ok, dev_ok, final_ok = (sem(n) for n in ("y_step", "var_ok", "dev_ok", "final_ok"))
    STEPS = 11

    def spread(b):
        return b[:].rearrange("p (k n) -> p k n", k=KC)[:, :, 0:NPB]

    block = ctx.enter_context(nc.Block())

    @block.sync
    def _(sp):
        for i, m in enumerate(mats):
            sp.dma_start(m_f[i][:], chunked(m)).then_inc(mat_in, 16)
        sp.wait_ge(zeroed, 1)
        for i, name in enumerate(("node_r1", "node_r2", "node_count")):
            sp.dma_start(row_fold[i:i + 1, :], rows(scratch[name])).then_inc(row_in, 16)
        for to, name in ((b1, "node_b1"), (gain, "node_g"), (shift, "node_beta")):
            sp.dma_start(to[:], rows(t["L1_gnn_" + name]).broadcast_to([NPB, D])).then_inc(row_in, 16)

        def tiles(i):
            for u in range(2):
                n = 2 * i + u
                need(sp, final_ok, n - 1)
                sp.dma_start(own[u][:], node_rows(scratch["node_own"], n)).then_inc(tile_in[u], 16)
                sp.dma_start(x1[u][:], node_rows(scratch["x1"], n)).then_inc(tile_in[u], 16)
            for u in range(2):
                n = 2 * i + u
                sp.wait_ge(final_ok, n + 1)
                sp.dma_start(node_rows(out_dram, n), final[u][:]).then_inc(stored[u], 16)

        pairs(sp, tiles)
        for u in range(2):
            sp.wait_ge(stored[u], 16 * NB // 2)

    @block.gpsimd
    def _(pool):
        pool.memset(row_fold[:], 0.0).then_inc(zeroed, 1)

        def tiles(i):
            for u in range(2):
                for norm in range(2):
                    m = 2 * (2 * i + u) + norm
                    pool.wait_ge(var_ok, m + 1)
                    pool.tensor_tensor(dev[:, 1:2], dev[:, 0:1], k["half"][0:NPB, :], ALU.pow).then_inc(dev_ok, 1)

        pairs(pool, tiles)

    @block.vector
    def _(dve):
        for i in range(3):
            dve.wait_ge(mat_hi_ok, i + 1)
            dve.tensor_tensor(m_lo[i][:], m_f[i][:], m_hi[i][:].bitcast(F32), ALU.subtract).then_inc(mat_ok, 1)

        def low_sums(n):
            need(dve, hidden_mm, n)
            dve.wait_ge(r_turned, n + 1)
            dve.tensor_copy(r_t[:], small_bank[0:4, 0:NPB]).then_inc(r_t_ok, 1)
            for j in range(2):
                dve.wait_ge(s_hi_ok, 2 * n + j + 1)
                dve.tensor_tensor(s_lo[j][:, :, 0:NPB], spread(turn_bank[j]), s_hi[j][:, :, 0:NPB].bitcast(F32),
                                  ALU.subtract).then_inc(s_lo_ok, 1)

        def tiles(i):
            for u in range(2):
                n = 2 * i + u
                dve.wait_ge(hidden_mm, n + 1)
                dve.wait_ge(tile_in[u], (n - u) * 16 + 32)
                dve.tensor_tensor(own[u][:], hidden_bank[0:NPB, :], own[u][:], ALU.add).then_inc(own_ok, 1)
                if not (isinstance(n, int) and n == NB - 1):
                    low_sums(n + 1)
                dve.wait_ge(nt_hi_ok, n + 1)
                dve.tensor_tensor(nt_lo[:, :, 0:NPB], spread(hturn_bank), nt_hi[:, :, 0:NPB].bitcast(F32),
                                  ALU.subtract).then_inc(nt_lo_ok, 1)
                at = [0]

                def done(ins):
                    at[0] += 1
                    ins.then_inc(y_step, 1)
                    dve.wait_ge(y_step, n * STEPS + at[0])

                dve.wait_ge(node_mm, n + 1)
                done(dve.tensor_tensor(y[:], node_bank[0:NPB, :], b1[:], ALU.add))
                done(dve.bn_stats(stats[:, 0:6], y[:]))
                dve.sem_inc(tick, 1)
                done(dve.bn_aggr(moments[:, 0:2], stats[:, 0:6]))
                dve.tensor_scalar(dev[:, 0:1], moments[:, 1:2], EPS, None, ALU.add).then_inc(var_ok, 1)
                dve.wait_ge(dev_ok, 2 * n + 1)
                done(dve.tensor_scalar(y[:], y[:], moments[:, 0:1], dev[:, 1:2], ALU.subtract, ALU.mult))
                done(dve.tensor_tensor(y[:], y[:], gain[:], ALU.mult))
                done(dve.tensor_tensor(y[:], y[:], shift[:], ALU.add))
                done(dve.tensor_tensor(y[:], y[:], x1[u][:], ALU.add))
                done(dve.tensor_tensor(y[:], y[:], x1[u][:], ALU.add))
                done(dve.bn_stats(stats[:, 0:6], y[:]))
                dve.sem_inc(tick, 1)
                done(dve.bn_aggr(moments[:, 0:2], stats[:, 0:6]))
                dve.tensor_scalar(dev[:, 0:1], moments[:, 1:2], EPS, None, ALU.add).then_inc(var_ok, 1)
                dve.wait_ge(dev_ok, 2 * n + 2)
                if not (isinstance(n, int) and n < 2):
                    dve.wait_ge(stored[u], (n - u) * 8)
                dve.tensor_scalar(final[u][:], y[:], moments[:, 0:1], dev[:, 1:2], ALU.subtract, ALU.mult).then_inc(final_ok, 1)
                done(dve.memset(stats[:], 0.0))
                assert at[0] == STEPS

        dve.wait_ge(row_in, 96)
        low_sums(0)
        pairs(dve, tiles)

    @block.scalar
    def _(act):
        for i in range(3):
            act.wait_ge(mat_in, 48)
            act.activation(m_hi[i][:], m_f[i][:], ACT.Copy).then_inc(mat_hi_ok, 1)

        def copy_sums(n, u):
            need(act, turned, 2 * (n - 1))
            need(act, r_turned, n - 1)
            for j, s in enumerate((k["sum_p"], k["sum_h"])):
                act.activation(s_in[j][u][:], tile_of(s, n)[0:NPB, :], ACT.Copy)
            act.activation(r_in[u][:], tile_of(k["sum_r"], n)[0:NPB, :], ACT.Copy).then_inc(copied, 1)

        def high_sums(n):
            need(act, hidden_mm, n)
            for j in range(2):
                act.wait_ge(turned, 2 * n + j + 1)
                act.activation(s_hi[j][:, :, 0:NPB], spread(turn_bank[j]), ACT.Copy).then_inc(s_hi_ok, 1)

        def tiles(i):
            for u in range(2):
                n = 2 * i + u
                last = isinstance(n, int) and n == NB - 1
                if not last:
                    copy_sums(n + 1, 1 - u)
                act.wait_ge(own_ok, n + 1)
                act.activation(hidden[:], own[u][:], ACT.Silu).then_inc(hidden_ok, 1)
                if not last:
                    high_sums(n + 1)
                act.wait_ge(hidden_turned, n + 1)
                need(act, node_mm, n)
                act.activation(nt_hi[:, :, 0:NPB], spread(hturn_bank), ACT.Copy).then_inc(nt_hi_ok, 1)

        copy_sums(0, 0)
        high_sums(0)
        pairs(act, tiles)

    @block.tensor
    def _(pe):
        def turn_sums(n, u):
            pe.wait_ge(copied, n + 1)
            need(pe, s_lo_ok, 2 * n)
            need(pe, r_t_ok, n)
            for j in range(2):
                for c in range(KC):
                    last = pe.transpose(turn_bank[j][:, c * P:c * P + NPB], s_in[j][u][:, c * P:(c + 1) * P], k["ident"][0:NPB, 0:NPB])
                last.then_inc(turned, 1)
            pe.matmul(small_bank[0:4, 0:NPB], r_in[u][:], k["ident"][0:NPB, 0:NPB], start=True, stop=True).then_inc(r_turned, 1)

        def tiles(i):
            for u in range(2):
                n = 2 * i + u
                pe.wait_ge(s_lo_ok, 2 * n + 2)
                pe.wait_ge(r_t_ok, n + 1)
                need(pe, own_ok, n)
                out = hidden_bank[0:NPB, :]
                pe.matmul(out, r_t[:], row_fold[:], start=True, stop=False, skip_group_check=True)
                for j in range(2):
                    for c in range(KC):
                        pe.matmul(out, s_hi[j][:, c, 0:NPB], m_hi[j][:, c, :], start=False, stop=False, skip_group_check=True)
                        pe.matmul(out, s_hi[j][:, c, 0:NPB], m_lo[j][:, c, :], start=False, stop=False, skip_group_check=True)
                        last = pe.matmul(out, s_lo[j][:, c, 0:NPB], m_hi[j][:, c, :], start=False,
                                         stop=(j == 1 and c == KC - 1), skip_group_check=True)
                last.then_inc(hidden_mm, 1)
                if not (isinstance(n, int) and n == NB - 1):
                    turn_sums(n + 1, 1 - u)
                pe.wait_ge(hidden_ok, n + 1)
                need(pe, nt_lo_ok, n)
                for c in range(KC):
                    last = pe.transpose(hturn_bank[:, c * P:c * P + NPB], hidden[:, c * P:(c + 1) * P], k["ident"][0:NPB, 0:NPB])
                last.then_inc(hidden_turned, 1)
                pe.wait_ge(nt_lo_ok, n + 1)
                need(pe, y_step, (n - 1) * STEPS + 1)
                product(pe, node_bank[0:NPB, :], (lambda c: nt_hi[:, c, 0:NPB], lambda c: nt_lo[:, c, 0:NPB]),
                        (lambda c: m_hi[2][:, c, :], lambda c: m_lo[2][:, c, :]), range(KC)).then_inc(node_mm, 1)

        turn_sums(0, 0)
        pe.wait_ge(mat_ok, 3)
        pe.wait_ge(row_in, 96)
        pairs(pe, tiles)


SCRATCH = {"records": (P * TILES, REC), "mesh_table": (N, D), "dst_table": (N, D), "x1": (N, D), "node_own": (N, D),
           "square1": (D, D), "fold_edge": (D, D), "square2": (D, D), "fold_node1": (D, D), "fold_node2": (D, D),
           "lin1": (D,), "fold_edge_b": (D,), "lin2": (D,), "edge_shift": (D,), "node_r1": (D,), "node_r2": (D,),
           "node_count": (D,)}
KEEP = {"ident": ([P, P], F32), "grid": ([P, P], F32), "half": ([P, 1], F32), "zeros": ([P, 16], F32),
        "floor": ([P, 2], F32), "recs": ([P, TILES, REC], F32),
        "tile_last": ([P, TILES], I32), "tile_bucket1": ([P, TILES], I32),
        "bucket_end": ([P, NB], I32)}
KEEP_AB = {"adj": ([P, NB, NB * P], I16), "degree": ([P, NB], F32)}
KEEP_CD = {"sum_p": ([P, NB, D], F32), "sum_h": ([P, NB, D], F32), "sum_r": ([P, NB, 4], F32)}


def build(nc, t, outs):
    with ExitStack() as whole:
        scratch = {n: nc.dram_tensor("s_" + n, list(s), F32, kind="Internal").ap() for n, s in SCRATCH.items()}
        keep = {n: whole.enter_context(nc.sbuf_tensor("k_" + n, s, d)) for n, (s, d) in KEEP.items()}
        with ExitStack() as both:
            keep.update({n: both.enter_context(nc.sbuf_tensor("k_" + n, s, d)) for n, (s, d) in KEEP_AB.items()})
            for phase in (phase_a, phase_b):
                with ExitStack() as ctx:
                    phase(nc, ctx, t, scratch, keep)
        keep.update({n: whole.enter_context(nc.sbuf_tensor("k_" + n, s, d)) for n, (s, d) in KEEP_CD.items()})
        with ExitStack() as ctx:
            phase_c(nc, ctx, t, scratch, keep)
        with ExitStack() as ctx:
            phase_d(nc, ctx, t, scratch, keep, outs[0])


_OUTS = [((N, D), "float32")]


def kernel(**inputs):
    import numpy as _np
    import concourse.bacc as _bacc
    from concourse import mybir as _mybir
    from concourse.bass_utils import run_bass_kernel_spmd as _run

    nc = _bacc.Bacc("TRN2", target_bir_lowering=False, num_devices=1)
    arrays, tensors, outs = {}, {}, []
    for name, a in inputs.items():
        a = _np.ascontiguousarray(a)
        arrays[f"in_{name}_dram"] = a
        tensors[name] = nc.dram_tensor(f"in_{name}_dram", a.shape, _mybir.dt.from_np(a.dtype), kind="ExternalInput").ap()
    for i, (shape, dtype) in enumerate(_OUTS):
        dt = _mybir.dt.from_np(_np.dtype(dtype))
        outs.append(nc.dram_tensor(f"out_{i}_dram", shape, dt, kind="ExternalOutput").ap())
    build(nc, tensors, outs)
    r = _run(nc, [arrays], core_ids=[0])
    got = tuple(r.results[0][f"out_{i}_dram"] for i in range(len(_OUTS)))
    return got if len(got) > 1 else got[0]
```

```python
from contextlib import ExitStack

import concourse.bass as bass
from concourse import mybir

F32 = mybir.dt.float32
F32R = mybir.dt.float32r
BF16 = mybir.dt.bfloat16
I32 = mybir.dt.int32
I16 = mybir.dt.int16
ALU = mybir.AluOpType
ACT = mybir.ActivationFunctionType
AX = mybir.AxisListType
ds = bass.ds

P = 128
N = 1250
E = 21250
D = 512
A4 = 4
KC = D // P
NB = 10
NPB = N // NB
EP, EC = 125, E // 125
TILES = (E + NB * P) // P
REC = 8
F_DST, F_SRC, F_DSTG, F_ATTR = 0, 1, 2, 3
STK = 32
EPS = 1e-5
SCAT = 17
GROUP = 4
GROUPS = TILES // GROUP
SQUARE_BLOCKS = (slice(0, 3), slice(1, 4), slice(2, 4), slice(0, 4, 3))
assert TILES % GROUP == 0 and EC % (2 * SCAT) == 0 and NPB * NB == N and EP * EC == E


def product(pe, out, lhs, rhs, chunks):
    for i, k in enumerate(chunks):
        pe.matmul(out, lhs[0](k), rhs[0](k), start=(i == 0), stop=False, skip_group_check=True)
        pe.matmul(out, lhs[0](k), rhs[1](k), start=False, stop=False, skip_group_check=True)
        last = pe.matmul(out, lhs[1](k), rhs[0](k), start=False, stop=(i == len(chunks) - 1),
                         skip_group_check=True)
    return last


class Chain:

    def __init__(self, engine, sem):
        self.engine, self.sem, self.n = engine, sem, 0

    def after(self, ins):
        self.n += 1
        ins.then_inc(self.sem, 1)
        self.engine.wait_ge(self.sem, self.n)


def rows(vector):
    return vector.rearrange("(a n) -> a n", a=1)


def columns(vector):
    return vector.rearrange("(k p) -> p k", p=P)


def chunked(matrix):
    return matrix.rearrange("(k p) n -> p k n", p=P)


def phase_a(nc, ctx, t, scratch, keep):
    def sb(name, shape, dt=F32):
        return ctx.enter_context(nc.sbuf_tensor("a_" + name, shape, dt))

    def sem(name):
        semaphores.append(nc.alloc_semaphore("a_" + name))
        return semaphores[-1]

    semaphores = []

    bank = [ctx.enter_context(nc.psum_tensor(f"a_bank{i}", [P, 512], F32)) for i in range(8)]
    src_i, dst_i = sb("src_i", [EP, EC], I32), sb("dst_i", [EP, EC], I32)
    attr_in = sb("attr_in", [EP, EC * A4])
    dst_f, bucket, where = (sb(n, [EP, EC]) for n in ("dst_f", "bucket", "where"))
    zero = sb("zero", [EP, EC])
    mask, scan = sb("mask", [EP, NB, EC]), sb("scan", [EP, NB, EC])
    totals, offset = sb("totals", [EP, NB]), sb("offset", [EP, NB])
    slot_i, slot_lo, slot_hi = (sb(n, [EP, EC], I32) for n in ("slot_i", "slot_lo", "slot_hi"))
    row_i = sb("row_i", [EP, EC], I32)
    record = sb("record", [EP, EC, REC])
    counts, tiles_f, ends, starts = (sb(n, [P, NB]) for n in ("counts", "tiles_f", "ends", "starts"))
    counts_i = sb("counts_i", [P, NB], I32)
    tile_no, tile_bucket = sb("tile_no", [P, TILES + 1]), sb("tile_bucket", [P, TILES + 1])
    tile_step, tile_flag = sb("tile_step", [P, TILES]), sb("tile_flag", [P, TILES])
    before, ones = sb("before", [P, P]), sb("ones", [P, P])
    pads = sb("pads", [P, TILES * REC])
    stage_row = [sb(f"stage_row{i}", [EP, SCAT], I32) for i in range(2)]
    stage_rec = [sb(f"stage_rec{i}", [EP, SCAT, REC]) for i in range(2)]
    w1t = [sb(f"w1t_{i}", [P, KC, D]) for i in range(2)]
    w1gt = [sb(f"w1gt_{i}", [P, KC, D]) for i in range(2)]
    w0a, w0b, wnb = (sb(n, [P, KC, D]) for n in ("w0a", "w0b", "wnb"))
    vecs = [sb(f"vecs_{i}", [P, 3, KC]) for i in range(2)]
    cols = [sb(f"cols_{i}", [P, 4, KC]) for i in range(2)]
    shift_sum = sb("shift_sum", [P, KC])
    mean = sb("mean", [P, 2, KC])
    bsum = sb("bsum", [P, 2])
    jobs_out = [sb(f"jobs_out{i}", [P, D]) for i in range(2)]
    rows_out = [sb(f"rows_out{i}", [1, D]) for i in range(2)]
    mesh = [sb(f"mesh{i}", [NPB, D]) for i in range(2)]
    mesh_t = [sb(f"mesh_t{i}", [P, KC, P]) for i in range(2)]
    mesh_out = [sb(f"mesh_out{i}", [NPB, D]) for i in range(2)]
    src_grid, dst_grid = sb("src_grid", [P, NB * P], I16), sb("dst_grid", [P, P], I16)
    ones16, zeros16 = sb("ones16", [P, 2], BF16), sb("zeros16", [P, 512], BF16)
    with ExitStack() as early:
        w1 = [early.enter_context(nc.sbuf_tensor(f"a_w1_{i}", [P, KC, D], F32)) for i in range(2)]
    hot_src = [sb(f"hot_src{i}", [P, NB * P], BF16) for i in range(GROUP)]
    hot_dst = [sb(f"hot_dst{i}", [P, P], BF16) for i in range(GROUP)]
    k, recs = keep, keep["recs"]

    edges_in, weights_in, vecs_in = sem("edges_in"), sem("weights_in"), sem("vecs_in")
    pool_const, dve_const = sem("pool_const"), sem("dve_const")
    pads_out, dve_chain = sem("pads_out"), sem("dve_chain")
    totals_ok, totals_mm, rows_ok, tables_ok = (sem(n) for n in ("totals_ok", "totals_mm", "rows_ok", "tables_ok"))
    staged, tick = sem("staged"), sem("tick")
    scattered = [sem(f"scattered{i}") for i in range(2)]
    recs_in, next_in = sem("recs_in"), sem("next_in")
    centred, turned, turned_out, gains_ok, bias_mm, cols_ok = (
        sem(n) for n in ("centred", "turned", "turned_out", "gains_ok", "bias_mm", "cols_ok"))
    job_mm, job_out_ok, square_mm = (sem(n) for n in ("job_mm", "job_out_ok", "square_mm"))
    row_out_ok = sem("row_out_ok")
    job_out = [sem(f"job_out{i}") for i in range(2)]
    mesh_in = [sem(f"mesh_in{i}") for i in range(2)]
    mesh_stored = [sem(f"mesh_stored{i}") for i in range(2)]
    mesh_turned, mesh_t_ok, mesh_mm, mesh_ok = (sem(n) for n in ("mesh_turned", "mesh_t_ok", "mesh_mm", "mesh_ok"))
    hot_ok, count_mm = sem("hot_ok"), sem("count_mm")
    copied_out = sem("copied_out")
    gate = [sem(f"gate{i}") for i in range(2)]

    def open_gates(engine, u):
        engine.wait_ge(tables_ok, 1)
        with engine.Fori(0, TILES // 2) as i:
            engine.wait_ge(copied_out, engine.value_load(k["tile_bucket1"][0:1, ds(2 * i + u, 1)], min_val=1, max_val=NB))
            engine.sem_inc(gate[u], 1)

    matrices = [("square1", w1t[0], w1t[0]), ("fold_edge", w1gt[0], w0a), ("square2", w1t[1], w1t[1]),
                ("fold_node1", w1gt[0], wnb), ("fold_node2", w1gt[1], wnb)]
    vectors = [("lin1", cols[0][:, 0], w1t[0]), ("fold_edge_b", cols[0][:, 1], w0a), ("lin2", cols[1][:, 0], w1t[1]),
               ("edge_shift", cols[0][:, 2], w0a), ("node_r1", cols[0][:, 1], wnb),
               ("node_r2", cols[1][:, 1], wnb), ("node_count", shift_sum, wnb)]
    NJ = len(matrices) * KC

    ctx.callback(nc.all_engine_barrier)
    ctx.callback(lambda: nc.clear_and_free_semaphores(semaphores))
    block = ctx.enter_context(nc.Block())

    @block.sync
    def _(sp):
        sp.dma_start(dst_i[:], t["dst"].rearrange("(p j) -> p j", p=EP)).then_inc(edges_in, 16)
        sp.dma_start(src_i[:], t["src"].rearrange("(p j) -> p j", p=EP)).then_inc(edges_in, 16)
        sp.dma_start(attr_in[:], t["edge_attr_4"].rearrange("(p j) a -> p (j a)", p=EP)).then_inc(edges_in, 16)
        sp.wait_ge(dve_const, 3)
        sp.dma_start(scratch["records"].rearrange("(p t) f -> p (t f)", p=P), pads[:]).then_inc(pads_out, 16)
        sp.dma_start(w1[0][:], chunked(t["L1_gnn_emb_W1"])).then_inc(weights_in, 16)
        sp.dma_start(w1[1][:], chunked(t["L1_gnn_edge_W1"])).then_inc(weights_in, 16)
        sp.dma_start(w0a[:], chunked(t["L1_gnn_edge_W0"][0:D, :])).then_inc(weights_in, 16)
        sp.dma_start(w0b[:], chunked(t["L1_gnn_edge_W0"][D:2 * D, :])).then_inc(weights_in, 16)
        sp.dma_start(wnb[:], chunked(t["L1_gnn_node_W0"][D:2 * D, :])).then_inc(weights_in, 16)
        for i, names in enumerate((("emb_b1", "emb_g", "emb_b"), ("edge_b1", "edge_g", "edge_beta"))):
            for j, name in enumerate(names):
                sp.dma_start(vecs[i][:, j, :], columns(t["L1_gnn_" + name]),
                             allow_slow_non_contiguous=True).then_inc(vecs_in, 16)
        for n in range(2):
            sp.dma_start(mesh[n][:], t["L1_gnn_mesh_nfeat"][n * NPB:(n + 1) * NPB, :]).then_inc(mesh_in[n], 16)
        sp.dma_start(k["h"][:], t["x"].rearrange("(b p) d -> p b d", p=NPB)).then_inc(next_in, 16)
        sp.dma_start(k["w0"][:], chunked(t["L0_gnn_Ws_self"][0])).then_inc(next_in, 16)
        sp.dma_start(k["w1"][:], chunked(t["L0_gnn_Ws_neigh"][0])).then_inc(next_in, 16)
        for j in range(NJ):
            name, i = matrices[j // KC][0], j % KC
            sp.wait_ge(job_out_ok, j + 1)
            sp.dma_start(scratch[name][i * P:(i + 1) * P, :], jobs_out[j % 2][:]).then_inc(job_out[j % 2], 16)
        for r in range(len(vectors)):
            sp.wait_ge(row_out_ok, r + 1)
            sp.dma_start(rows(scratch[vectors[r][0]]), rows_out[r % 2][:]).then_inc(job_out[r % 2], 16)
        with sp.Fori(0, NB // 2 - 1) as i:
            for u in range(2):
                sp.wait_ge(mesh_turned, 2 * i + u + 1)
                sp.dma_start(mesh[u][:], t["L1_gnn_mesh_nfeat"][ds((2 * i + 2 + u) * NPB, NPB), :]).then_inc(mesh_in[u], 16)
            for u in range(2):
                sp.wait_ge(mesh_ok, 2 * i + u + 1)
                sp.dma_start(scratch["mesh_table"][ds((2 * i + u) * NPB, NPB), :], mesh_out[u][:]).then_inc(mesh_stored[u], 16)
        for u in range(2):
            n = NB - 2 + u
            sp.wait_ge(mesh_ok, n + 1)
            sp.dma_start(scratch["mesh_table"][n * NPB:(n + 1) * NPB, :], mesh_out[u][:]).then_inc(mesh_stored[u], 16)
        for u in range(2):
            sp.wait_ge(scattered[u], 16 * EC // 2)
        sp.dma_start(recs[:], scratch["records"].rearrange("(p t) f -> p t f", p=P)).then_inc(recs_in, 16)
        for u in range(2):
            sp.wait_ge(job_out[u], 16 * (NJ // 2) + 16 * ((len(vectors) + 1 - u) // 2))
            sp.wait_ge(mesh_stored[u], 16 * NB // 2)
        sp.wait_ge(next_in, 48)
        open_gates(sp, 0)

    @block.gpsimd
    def _(pool):
        pool.iota(dst_grid[:], [[1, P]], base=0, channel_multiplier=0).then_inc(pool_const, 1)
        pool.iota(src_grid[:], [[NPB, NB], [1, P]], base=0, channel_multiplier=0).then_inc(pool_const, 1)
        pool.iota(tile_no[:], [[1, TILES + 1]], base=0, channel_multiplier=0,
                  allow_small_or_imprecise_dtypes=True).then_inc(pool_const, 1)
        pool.iota(k["grid"][:], [[1, P]], base=0, channel_multiplier=0,
                  allow_small_or_imprecise_dtypes=True).then_inc(pool_const, 1)
        pool.wait_ge(dve_const, 2)
        pool.affine_select(out=k["ident"][:], in_=k["ident"][:], compare_op=ALU.not_equal, fill=1.0, base=0,
                           pattern=[[-1, P]], channel_multiplier=1).then_inc(pool_const, 1)
        pool.affine_select(out=before[:], in_=before[:], compare_op=ALU.is_gt, fill=0.0, base=0,
                           pattern=[[1, P]], channel_multiplier=-1).then_inc(pool_const, 1)
        def stage(u, j, fixed):
            at = slice((2 * j + u) * SCAT, (2 * j + u + 1) * SCAT) if fixed else ds((2 * j + u) * SCAT, SCAT)
            if not fixed:
                pool.wait_ge(scattered[u], j * (16 * SCAT))
                pool.sem_inc(tick, 1)
            pool.tensor_copy(stage_row[u][:], row_i[:, at]).then_inc(staged, 1)
            pool.tensor_copy(stage_rec[u][:], record[:, at, :]).then_inc(staged, 1)
            pool.wait_ge(staged, (2 * j + u + 1) * 2)
            if not fixed:
                pool.sem_inc(tick, 1)
            for c in range(SCAT):
                pool.indirect_dma_start(scratch["records"], bass.IndirectOffsetOnAxis(ap=stage_row[u][:, c:c + 1], axis=0),
                                        stage_rec[u][:, c, :], None).then_inc(scattered[u], 16)

        pool.wait_ge(pads_out, 16)
        pool.wait_ge(rows_ok, 1)
        for u in range(2):
            stage(u, 0, True)
        with pool.Fori(1, EC // (2 * SCAT)) as j:
            for u in range(2):
                stage(u, j, False)
        open_gates(pool, 1)

    @block.vector
    def _(dve):
        chain = Chain(dve, dve_chain)
        dve.memset(k["ident"][:], 0.0).then_inc(dve_const, 1)
        dve.memset(before[:], 1.0).then_inc(dve_const, 1)
        chain.after(dve.memset(pads[:], 0.0))
        dve.memset(pads[:].rearrange("p (t f) -> p t f", f=REC)[:, :, F_DST:F_DST + 1], -1.0).then_inc(dve_const, 1)
        dve.memset(ones[:], 1.0).then_inc(dve_const, 1)
        dve.memset(ones16[:], 1.0).then_inc(dve_const, 1)
        dve.memset(zeros16[:], 0.0).then_inc(dve_const, 1)
        dve.memset(zero[:], 0.0)
        dve.memset(record[:, :, F_ATTR + A4:], 0.0)
        dve.memset(k["half"][:], -0.5)
        dve.memset(k["zeros"][:], 0.0)
        dve.wait_ge(edges_in, 48)
        chain.after(dve.tensor_copy(dst_f[:], dst_i[:]))
        dve.tensor_copy(record[:, :, F_SRC], src_i[:])
        dve.tensor_copy(record[:, :, F_ATTR:F_ATTR + A4], attr_in[:].rearrange("p (j a) -> p j a", a=A4))
        dve.tensor_copy(record[:, :, F_DSTG], dst_f[:])
        chain.after(dve.tensor_scalar(bucket[:], dst_f[:], float(NPB), None, ALU.is_ge))
        for c in range(2, NB):
            chain.after(dve.scalar_tensor_tensor(out=bucket[:], in0=dst_f[:], scalar=float(c * NPB), in1=bucket[:],
                                                 op0=ALU.is_ge, op1=ALU.add))
        dve.scalar_tensor_tensor(out=record[:, :, F_DST], in0=bucket[:], scalar=-float(NPB), in1=dst_f[:],
                                 op0=ALU.mult, op1=ALU.add)
        for c in range(NB):
            last = dve.tensor_scalar(mask[:, c, :], bucket[:], float(c), None, ALU.is_equal)
        chain.after(last)
        for c in range(NB):
            last = dve.tensor_tensor_scan(out=scan[:, c, :], data0=mask[:, c, :], data1=zero[:], initial=0.0,
                                          op0=ALU.add, op1=ALU.add)
        chain.after(last)
        dve.tensor_copy(totals[:], scan[:, :, EC - 1]).then_inc(totals_ok, 1)
        dve.wait_ge(totals_mm, 1)
        chain.after(dve.tensor_scalar(counts[:], bank[1][:, 0:NB], float(P - 1), None, ALU.add))
        chain.after(dve.tensor_copy(counts_i[:], counts[:]))
        chain.after(dve.tensor_scalar(counts_i[:], counts_i[:], 7, None, ALU.logical_shift_right))
        chain.after(dve.tensor_copy(tiles_f[:], counts_i[:]))
        chain.after(dve.tensor_scalar(tiles_f[:], tiles_f[:], 1.0, None, ALU.max))
        chain.after(dve.tensor_tensor_scan(out=ends[:], data0=tiles_f[:], data1=k["zeros"][:, 0:NB],
                                           initial=0.0, op0=ALU.add, op1=ALU.add))
        chain.after(dve.tensor_tensor(starts[:], ends[:], tiles_f[:], ALU.subtract))
        chain.after(dve.tensor_scalar(offset[:], starts[0:EP, :], float(P), -1.0, ALU.mult, ALU.add))
        chain.after(dve.tensor_tensor(offset[:], offset[:], bank[0][0:EP, 0:NB], ALU.add))
        for c in range(NB):
            last = dve.scalar_tensor_tensor(out=scan[:, c, :], in0=scan[:, c, :], scalar=offset[:, c:c + 1], in1=mask[:, c, :],
                                            op0=ALU.add, op1=ALU.mult)
        chain.after(last)
        chain.after(dve.tensor_reduce(where[:], scan[:].rearrange("p c j -> p j c"), AX.X, ALU.add))
        chain.after(dve.tensor_copy(slot_i[:], where[:]))
        dve.tensor_scalar(slot_lo[:], slot_i[:], P - 1, None, ALU.bitwise_and)
        chain.after(dve.tensor_scalar(slot_hi[:], slot_i[:], 7, None, ALU.logical_shift_right))
        chain.after(dve.scalar_tensor_tensor(out=row_i[:], in0=slot_lo[:], scalar=float(TILES), in1=slot_hi[:],
                                             op0=ALU.mult, op1=ALU.add))
        dve.sem_inc(rows_ok, 1)
        dve.wait_ge(pool_const, 6)
        chain.after(dve.tensor_scalar(tile_bucket[:], tile_no[:], starts[:, 1:2], None, ALU.is_ge))
        for c in range(2, NB):
            chain.after(dve.scalar_tensor_tensor(out=tile_bucket[:], in0=tile_no[:], scalar=starts[:, c:c + 1], in1=tile_bucket[:],
                                                 op0=ALU.is_ge, op1=ALU.add))
        chain.after(dve.memset(tile_bucket[:, TILES:], float(NB)))
        chain.after(dve.tensor_tensor(tile_step[:], tile_bucket[:, 1:], tile_bucket[:, :TILES], ALU.subtract))
        chain.after(dve.scalar_tensor_tensor(out=tile_flag[:], in0=tile_bucket[:, :TILES], scalar=1.0, in1=tile_step[:],
                                             op0=ALU.add, op1=ALU.mult))
        dve.tensor_copy(k["tile_last"][:], tile_flag[:])
        dve.tensor_scalar(k["tile_bucket1"][:], tile_bucket[:, :TILES], 1.0, None, ALU.add)
        dve.tensor_copy(k["bucket_end"][:], ends[:]).then_inc(tables_ok, 1)
        dve.wait_ge(weights_in, 80)
        dve.wait_ge(vecs_in, 96)
        for i in range(2):
            chain.after(dve.tensor_reduce(mean[:, i, :], w1[i][:], AX.X, ALU.add))
            chain.after(dve.tensor_scalar(mean[:, i, :], mean[:, i, :], 1.0 / D, None, ALU.mult))
            for c in range(KC):
                last = dve.tensor_scalar(w1[i][:, c, :], w1[i][:, c, :], mean[:, i, c:c + 1], None, ALU.subtract)
            last.then_inc(centred, 1)
            chain.after(dve.tensor_reduce(bsum[:, i:i + 1], vecs[i][:, 0, :], AX.X, ALU.add))
        dve.sem_inc(centred, 1)
        dve.wait_ge(bias_mm, 1)
        chain.after(dve.tensor_scalar(bsum[:], bank[2][:, 0:2], 1.0 / D, None, ALU.mult))
        for i in range(2):
            chain.after(dve.tensor_scalar(vecs[i][:, 0, :], vecs[i][:, 0, :], bsum[:, i:i + 1], None, ALU.subtract))
            dve.tensor_scalar(cols[i][:, 0, :], vecs[i][:, 0, :], 2.0, None, ALU.mult)
            dve.tensor_tensor(cols[i][:, 1, :], vecs[i][:, 0, :], vecs[i][:, 1, :], ALU.mult)
            dve.tensor_copy(cols[i][:, 2, :], vecs[i][:, 2, :])
            dve.tensor_tensor(cols[i][:, 3, :], vecs[i][:, 0, :], vecs[i][:, 0, :], ALU.mult)
        dve.tensor_tensor(shift_sum[:], vecs[0][:, 2, :], vecs[1][:, 2, :], ALU.add).then_inc(cols_ok, 1)
        for i in range(2):
            for o in range(KC):
                dve.wait_ge(turned, KC * i + o + 1)
                chain.after(dve.tensor_copy(w1t[i][:, o, :], bank[4 + o][:]))
                dve.sem_inc(turned_out, 1)
                last = dve.tensor_scalar(w1gt[i][:, o, :], w1t[i][:, o, :], vecs[i][:, 1, o:o + 1], None, ALU.mult)
            last.then_inc(gains_ok, 1)
        dve.wait_ge(square_mm, 1)
        dve.tensor_scalar(k["floor"][:], bank[3][:, 0:2], 1.0 / D, EPS, ALU.mult, ALU.add).then_inc(dve_const, 1)
        def mesh_copy(n, u, fixed):
            if not fixed:
                dve.wait_ge(mesh_stored[u], (n - u) * 8)
            dve.wait_ge(mesh_mm, n + 1)
            dve.tensor_copy(mesh_out[u][:], bank[6 + u][0:NPB, :]).then_inc(mesh_ok, 1)

        for u in range(2):
            mesh_copy(u, u, True)
        with dve.Fori(1, NB // 2) as i:
            for u in range(2):
                mesh_copy(2 * i + u, u, False)
        dve.wait_ge(recs_in, 16)
        def field(n, f):
            return recs[:, n, f:f + 1] if isinstance(n, int) else recs[:, ds(n, 1), f:f + 1].rearrange("p a b -> p (a b)")

        def one_hot(n, u, fixed):
            if not fixed:
                dve.wait_ge(count_mm, n - GROUP + 1)
            dve.tensor_scalar(hot_src[u][:], src_grid[:], field(n, F_SRC), None, ALU.is_equal)
            dve.tensor_scalar(hot_dst[u][:], dst_grid[:], field(n, F_DST), None, ALU.is_equal).then_inc(hot_ok, 1)

        for u in range(GROUP):
            one_hot(u, u, True)
        with dve.Fori(1, GROUPS) as i:
            for u in range(GROUP):
                one_hot(GROUP * i + u, u, False)

    @block.scalar
    def _(act):
        for j in range(NJ):
            name, i = matrices[j // KC][0], j % KC
            act.wait_ge(job_mm, j + 1)
            if j >= 2:
                act.wait_ge(job_out[j % 2], 16 * (j // 2))
            if name.startswith("square"):
                for c in range(KC):
                    to = slice(c * P, (c + 1) * P)
                    last = act.activation(jobs_out[j % 2][:, to], bank[j % 2][:, to], ACT.Copy, scale=1.0 if c == i else 2.0)
            else:
                last = act.activation(jobs_out[j % 2][:], bank[j % 2][:], ACT.Copy)
            last.then_inc(job_out_ok, 1)
        for r in range(len(vectors)):
            act.wait_ge(job_mm, NJ + r + 1)
            act.wait_ge(job_out[r % 2], 16 * (NJ // 2) + 16 * (r // 2))
            act.activation(rows_out[r % 2][:], bank[r % 2][0:1, :], ACT.Copy).then_inc(row_out_ok, 1)
        def mesh_copy(n, u, fixed):
            if not fixed:
                act.wait_ge(mesh_mm, n - 1)
            act.wait_ge(mesh_turned, n + 1)
            act.activation(mesh_t[u][:, :, 0:NPB],
                           bank[4 + u][:].rearrange("p (k n) -> p k n", k=KC)[:, :, 0:NPB], ACT.Copy).then_inc(mesh_t_ok, 1)

        for u in range(2):
            mesh_copy(u, u, True)
        with act.Fori(1, NB // 2) as i:
            for u in range(2):
                mesh_copy(2 * i + u, u, False)
        act.wait_ge(tables_ok, 1)
        for c in range(NB):
            if c < NB - 1:
                act.wait_ge(count_mm, act.value_load(k["bucket_end"][0:1, c:c + 1], min_val=1, max_val=TILES))
            else:
                act.wait_ge(count_mm, TILES)
            for b in range(3):
                lo, hi = b * 512, min((b + 1) * 512, NB * P)
                act.activation(k["adj"][:, c, lo:hi], bank[b][:, 0:hi - lo], ACT.Copy)
            act.activation(k["degree"][:, c:c + 1], bank[3][:, 0:1], ACT.Copy).then_inc(copied_out, 1)

    @block.tensor
    def _(pe):
        pe.wait_ge(dve_const, 4)
        pe.wait_ge(pool_const, 6)
        pe.wait_ge(totals_ok, 1)
        pe.matmul(bank[0][0:EP, 0:NB], before[0:EP, 0:EP], totals[:], start=True, stop=True)
        pe.matmul(bank[1][:, 0:NB], ones[0:EP, :], totals[:], start=True, stop=True).then_inc(totals_mm, 1)
        pe.wait_ge(centred, 3)
        pe.matmul(bank[2][:, 0:2], ones[:], bsum[:], start=True, stop=True).then_inc(bias_mm, 1)
        for i in range(2):
            for o in range(KC):
                if i:
                    pe.wait_ge(turned_out, o + 1)
                for c in range(KC):
                    last = pe.transpose(bank[4 + o][:, c * P:(c + 1) * P], w1[i][:, c, o * P:(o + 1) * P], k["ident"][:])
                last.then_inc(turned, 1)
        pe.wait_ge(cols_ok, 1)
        for i in range(2):
            for c in range(KC):
                last = pe.matmul(bank[3][:, i:i + 1], ones[:], cols[i][:, 3, c:c + 1], start=(c == 0), stop=(c == KC - 1),
                                 skip_group_check=True)
        last.then_inc(square_mm, 1)
        pe.wait_ge(gains_ok, 2)
        for j in range(NJ):
            _, left, right = matrices[j // KC]
            i = j % KC
            if j >= 2:
                pe.wait_ge(job_out_ok, j - 1)
            for c in range(KC):
                last = pe.matmul(bank[j % 2][:], left[:, c, i * P:(i + 1) * P], right[:, c, :],
                                 start=(c == 0), stop=(c == KC - 1))
            last.then_inc(job_mm, 1)
        for r in range(len(vectors)):
            _, left, right = vectors[r]
            if r < 2:
                pe.wait_ge(job_out_ok, NJ - 1 + r)
            else:
                pe.wait_ge(row_out_ok, r - 1)
            for c in range(KC):
                last = pe.matmul(bank[r % 2][0:1, :], left[:, c:c + 1], right[:, c, :], start=(c == 0), stop=(c == KC - 1))
            last.then_inc(job_mm, 1)
        def turn(n, u, fixed):
            pe.wait_ge(mesh_in[u], 16 if fixed else (n - u) * 8 + 16)
            if not fixed:
                pe.wait_ge(mesh_t_ok, n - 1)
            for c in range(KC):
                last = pe.transpose(bank[4 + u][:, c * P:c * P + NPB], mesh[u][:, c * P:(c + 1) * P], k["ident"][0:NPB, 0:NPB])
            last.then_inc(mesh_turned, 1)

        def multiply(n, u, fixed):
            pe.wait_ge(mesh_t_ok, n + 1)
            if not fixed:
                pe.wait_ge(mesh_ok, n - 1)
            for c in range(KC):
                last = pe.matmul(bank[6 + u][0:NPB, :], mesh_t[u][:, c, 0:NPB], w0b[:, c, :], start=(c == 0), stop=(c == KC - 1))
            last.then_inc(mesh_mm, 1)

        pe.wait_ge(turned_out, 2 * KC)
        for u in range(2):
            turn(u, u, True)
        for u in range(2):
            multiply(u, u, True)
        with pe.Fori(1, NB // 2) as i:
            for u in range(2):
                turn(2 * i + u, u, False)
            for u in range(2):
                multiply(2 * i + u, u, False)
        pe.wait_ge(dve_const, 7)
        pe.wait_ge(row_out_ok, len(vectors))
        pe.wait_ge(tables_ok, 1)
        for b in range(4):
            pe.matmul(bank[b][:], zeros16[:, 0:P], zeros16[:], start=True, stop=False, skip_group_check=True)

        def count(n, u, fixed):
            pe.wait_ge(hot_ok, n + 1)
            pe.wait_ge(gate[u % 2], n // 2 + 1 if fixed else (n - u % 2 + 2) // 2)
            for s in range(NB):
                pe.matmul(bank[s // 4][:, (s % 4) * P:(s % 4 + 1) * P], hot_src[u][:, s * P:(s + 1) * P], hot_dst[u][:],
                          start=False, stop=False, skip_group_check=True)
            pe.matmul(bank[3][:, 0:2], hot_dst[u][:], ones16[:], start=False, stop=False,
                      skip_group_check=True).then_inc(count_mm, 1)

        pe.sem_inc(copied_out, 1)
        for u in range(GROUP):
            count(u, u, True)
        with pe.Fori(1, GROUPS) as i:
            for u in range(GROUP):
                count(GROUP * i + u, u, False)


def need(engine, sem, value):
    if not isinstance(value, int) or value > 0:
        engine.wait_ge(sem, value)


def pairs(engine, body):
    body(0)
    with engine.Fori(1, NB // 2 - 1) as i:
        body(i)
    body(NB // 2 - 1)


def tile_of(tensor, n):
    return tensor[:, n, :] if isinstance(n, int) else tensor[:, ds(n, 1), :].rearrange("p a b -> p (a b)")


def node_rows(matrix, n):
    return matrix[n * NPB:(n + 1) * NPB, :] if isinstance(n, int) else matrix[ds(n * NPB, NPB), :]


LAYERS = 3
EXACT = 4096


def phase_b(nc, ctx, t, scratch, keep):
    def sb(name, shape, dt=F32):
        return ctx.enter_context(nc.sbuf_tensor("b_" + name, shape, dt))

    def sem(name):
        return ctx.enter_context(nc.semaphore("b_" + name))

    bank = [ctx.enter_context(nc.psum_tensor(f"b_bank{i}", [P, 512], F32)) for i in range(8)]
    turn_bank, self_bank, neigh_bank, sum_bank = bank[0:2], bank[2:4], bank[4:6], bank[6:8]
    h, w = keep["h"], [keep["w0"], keep["w1"]]
    u_hi, u_lo = sb("u_hi", [NPB, NB, D], F32R), sb("u_lo", [NPB, NB, D], F32R)
    w_hi = [sb(f"w_hi{i}", [P, KC, D], F32R) for i in range(2)]
    w_lo = [sb(f"w_lo{i}", [P, KC, D], F32R) for i in range(2)]
    bias = [sb(f"bias{i}", [NPB, D]) for i in range(2)]
    bias2 = sb("bias2", [NPB, D])
    hc = [sb(f"hc{i}", [NPB, D]) for i in range(2)]
    ht_hi = [sb(f"ht_hi{i}", [P, KC, P], F32R) for i in range(2)]
    ht_lo = [sb(f"ht_lo{i}", [P, KC, P], F32R) for i in range(2)]
    a_hi = [sb(f"a_hi{i}", [NPB, NB * P], F32R) for i in range(2)]
    a_lo = [sb(f"a_lo{i}", [NPB, NB * P], F32R) for i in range(2)]
    degree, inv_degree = sb("degree", [P, NB]), sb("inv_degree", [NPB, NB])
    mixed = [sb(f"mixed{i}", [NPB, D]) for i in range(2)]
    x = [sb(f"x{i}", [NPB, D]) for i in range(2)]
    out = [sb(f"out{i}", [NPB, 2, D]) for i in range(2)]
    most, many, many_i, ones = sb("most", [P, 1]), sb("many", [P, 2]), sb("many_i", [1, 2], I32), sb("ones", [P, 2])
    stats = [sb(f"stats{i}", [NPB, 6]) for i in range(2)]
    moments = [sb(f"moments{i}", [NPB, 2]) for i in range(2)]
    dev = [sb(f"dev{i}", [NPB, 2]) for i in range(2)]
    k = keep

    w_in, bias_in, w_hi_ok = sem("w_in"), sem("bias_in"), sem("w_hi_ok")
    counts_ok, self_split = sem("counts_ok"), sem("self_split")
    many_ok, many_mm, many_read = sem("many_ok"), sem("many_mm"), sem("many_read")
    w_split, split_step, chain_sem = sem("w_split"), sem("split_step"), sem("chain")
    hc_ok, turned, ht_hi_ok, ht_lo_ok, prod_mm = (
        sem(n) for n in ("hc_ok", "turned", "ht_hi_ok", "ht_lo_ok", "prod_mm"))
    self_ok, u_hi_ok, u_lo_ok = sem("self_ok"), sem("u_hi_ok"), sem("u_lo_ok")
    a_hi_ok, a_lo_ok, sum_mm, mixed_ok, h_ok = (sem(n) for n in ("a_hi_ok", "a_lo_ok", "sum_mm", "mixed_ok", "h_ok"))
    x_in = [sem(f"x_in{i}") for i in range(2)]
    res_ok, stats_ok, moments_ok, var_ok, dev_ok = (sem(n) for n in ("res_ok", "stats_ok", "moments_ok", "var_ok", "dev_ok"))
    tick = sem("tick")
    x1_stored = [sem(f"x1_stored{i}") for i in range(2)]
    stored = [sem(f"stored{i}") for i in range(2)]

    weights = [(t["L0_gnn_Ws_self"][q], t["L0_gnn_Ws_neigh"][q]) for q in range(LAYERS)]
    weights.append((t["L1_gnn_node_W0"][0:D, :], t["L1_gnn_edge_W0"][2 * D:3 * D, :]))
    PASSES = LAYERS + 1

    def column(tensor, n):
        return tensor[:, n:n + 1] if isinstance(n, int) else tensor[:, ds(n, 1)]

    def spread(b):
        return b[:].rearrange("p (k n) -> p k n", k=KC)[:, :, 0:NPB]

    block = ctx.enter_context(nc.Block())

    @block.sync
    def _(sp):
        for q in range(PASSES):
            if q:
                sp.wait_ge(w_split, q)
                for i in range(2):
                    sp.dma_start(w[i][:], chunked(weights[q][i])).then_inc(w_in, 16)
            if q < LAYERS:
                if q:
                    sp.wait_ge(self_ok, NB * q)
                sp.dma_start(bias[0][:], rows(t["L0_gnn_bs"][q]).broadcast_to([NPB, D])).then_inc(bias_in, 16)
        sp.wait_ge(self_ok, NB * LAYERS)
        sp.dma_start(bias[0][:], rows(t["L1_gnn_node_b0"]).broadcast_to([NPB, D])).then_inc(bias_in, 16)
        sp.dma_start(bias[1][:], rows(t["L1_gnn_edge_b0"]).broadcast_to([NPB, D])).then_inc(bias_in, 16)
        sp.dma_start(bias2[:], rows(scratch["edge_shift"]).broadcast_to([NPB, D])).then_inc(bias_in, 16)
        def residual(i):
            for u in range(2):
                n = 2 * i + u
                need(sp, res_ok, n - 1)
                sp.dma_start(x[u][:], node_rows(t["x"], n)).then_inc(x_in[u], 16)
            for u in range(2):
                n = 2 * i + u
                sp.wait_ge(h_ok, NB * (LAYERS - 1) + n + 1)
                sp.dma_start(node_rows(scratch["x1"], n), tile_of(h, n)).then_inc(x1_stored[u], 16)

        pairs(sp, residual)
        def results(i):
            for u in range(2):
                n = 2 * i + u
                sp.wait_ge(u_lo_ok, NB * LAYERS + n + 1)
                sp.dma_start(node_rows(scratch["node_own"], n), out[u][:, 0, :]).then_inc(stored[u], 16)
                sp.dma_start(node_rows(scratch["dst_table"], n), out[u][:, 1, :]).then_inc(stored[u], 16)

        pairs(sp, results)
        for u in range(2):
            sp.wait_ge(x1_stored[u], 16 * NB // 2)
            sp.wait_ge(stored[u], 32 * NB // 2)

    @block.gpsimd
    def _(pool):
        for q in range(1, PASSES):
            pool.wait_ge(w_in, 32 * q)
            pool.wait_ge(prod_mm, NB * q)
            for i in range(2):
                pool.tensor_copy(w_hi[i][:], w[i][:]).then_inc(split_step, 1)
            pool.wait_ge(split_step, 2 * q)
            pool.tensor_tensor(w_lo[0][:], w[0][:], w_hi[0][:].bitcast(F32), ALU.subtract)
            pool.tensor_tensor(w_lo[1][:], w[1][:], w_hi[1][:].bitcast(F32), ALU.subtract).then_inc(w_split, 1)

        def deviation(i):
            for u in range(2):
                n = 2 * i + u
                pool.wait_ge(var_ok, n + 1)
                pool.sem_inc(tick, 1)
                pool.tensor_tensor(dev[u][:, 1:2], dev[u][:, 0:1], k["half"][0:NPB, :], ALU.pow).then_inc(dev_ok, 1)

        pairs(pool, deviation)

    @block.vector
    def _(dve):
        chain = Chain(dve, chain_sem)
        dve.tensor_copy(degree[:, 0:1], k["degree"][:, 0:1])
        chain.after(dve.tensor_tensor(degree[:, 1:], k["degree"][:, 1:], k["degree"][:, 0:NB - 1], ALU.subtract))
        chain.after(dve.tensor_scalar(inv_degree[:], degree[0:NPB, :], 1.0, None, ALU.max))
        chain.after(dve.reciprocal(inv_degree[:], inv_degree[:]))

        counts = Chain(dve, counts_ok)

        def own_counts():
            for _ in range(3):
                c = NB - 1 - counts.n
                own = k["adj"][0:NPB, c, :]
                counts.after(dve.tensor_tensor(own, own, k["adj"][0:NPB, c - 1, :], ALU.subtract))

        def low(g, u):
            dve.wait_ge(ht_hi_ok, g + 1)
            need(dve, prod_mm, g - 1)
            dve.tensor_tensor(ht_lo[u][:, :, 0:NPB], spread(turn_bank[u]), ht_hi[u][:, :, 0:NPB].bitcast(F32),
                              ALU.subtract).then_inc(ht_lo_ok, 1)

        for q in range(PASSES):
            def evacuate(i, q=q):
                for u in range(2):
                    n = 2 * i + u
                    g = NB * q + n
                    if not (isinstance(n, int) and n == NB - 1):
                        low(g + 1, 1 - u)
                    dve.wait_ge(prod_mm, g + 1)
                    if q < LAYERS:
                        dve.tensor_tensor(tile_of(h, n), self_bank[u][0:NPB, :], bias[0][:], ALU.add).then_inc(self_ok, 1)
                        dve.wait_ge(u_hi_ok, g + 1)
                        dve.tensor_tensor(tile_of(u_lo, n), neigh_bank[u][0:NPB, :], tile_of(u_hi, n).bitcast(F32),
                                          ALU.subtract).then_inc(u_lo_ok, 1)
                        if q == 0 and isinstance(n, int) and n in (0, 1, NB - 2):
                            own_counts()
                    else:
                        if not (isinstance(n, int) and n < 2):
                            dve.wait_ge(stored[u], (n - u) * 16)
                        dve.tensor_tensor(out[u][:, 0, :], self_bank[u][0:NPB, :], bias[0][:], ALU.add)
                        dve.tensor_tensor(out[u][:, 1, :], neigh_bank[u][0:NPB, :], bias[1][:], ALU.add).then_inc(u_lo_ok, 1)

            dve.wait_ge(bias_in, 16 * (q + 1) if q < LAYERS else 16 * (q + 3))
            if q == LAYERS:
                chain.after(dve.tensor_tensor(bias[1][:], bias[1][:], bias2[:], ALU.add))
            if q == 0:
                for i in range(2):
                    dve.wait_ge(w_hi_ok, i + 1)
                    ins = dve.tensor_tensor(w_lo[i][:], w[i][:], w_hi[i][:].bitcast(F32), ALU.subtract)
                    if i == 0:
                        ins.then_inc(self_split, 1)
                        low(0, 0)
                ins.then_inc(w_split, 1)
            pairs(dve, evacuate)
            if q == LAYERS:
                break

            def rest(n, u, q=q):
                g = NB * q + n
                dve.wait_ge(a_hi_ok, g + 1)
                need(dve, sum_mm, g - 1)
                dve.tensor_tensor(a_lo[u][:], tile_of(k["adj"], n)[0:NPB, :], a_hi[u][:].bitcast(F32),
                                  ALU.subtract).then_inc(a_lo_ok, 1)

            def mix(i, q=q):
                for u in range(2):
                    n = 2 * i + u
                    g = NB * q + n
                    if not (isinstance(n, int) and n == NB - 1):
                        rest(n + 1, 1 - u)
                    else:
                        low(g + 1, 0)
                    dve.wait_ge(sum_mm, g + 1)
                    need(dve, h_ok, g - 1)
                    dve.scalar_tensor_tensor(out=mixed[u][:], in0=sum_bank[u][0:NPB, :], scalar=column(inv_degree, n),
                                             in1=tile_of(h, n), op0=ALU.mult, op1=ALU.add).then_inc(mixed_ok, 1)
                if q < LAYERS - 1:
                    return
                for u in range(2):
                    n = 2 * i + u
                    dve.wait_ge(x_in[u], (n - u) * 8 + 16)
                    dve.wait_ge(mixed_ok, NB * q + n + 1)
                    dve.tensor_tensor(mixed[u][:], mixed[u][:], x[u][:], ALU.add).then_inc(res_ok, 1)
                for u in range(2):
                    dve.wait_ge(res_ok, 2 * i + u + 1)
                    dve.bn_stats(stats[u][:], mixed[u][:]).then_inc(stats_ok, 1)
                for u in range(2):
                    dve.wait_ge(stats_ok, 2 * i + u + 1)
                    dve.sem_inc(tick, 1)
                    dve.bn_aggr(moments[u][:], stats[u][:]).then_inc(moments_ok, 1)
                for u in range(2):
                    dve.wait_ge(moments_ok, 2 * i + u + 1)
                    dve.tensor_scalar(dev[u][:, 0:1], moments[u][:, 1:2], EPS, None, ALU.add).then_inc(var_ok, 1)
                for u in range(2):
                    n = 2 * i + u
                    dve.wait_ge(dev_ok, n + 1)
                    dve.tensor_scalar(tile_of(h, n), mixed[u][:], moments[u][:, 0:1], dev[u][:, 1:2],
                                      ALU.subtract, ALU.mult).then_inc(h_ok, 1)

            rest(0, 0)
            if q == 0:
                dve.tensor_reduce(most[:], degree[:], AX.X, ALU.max).then_inc(many_ok, 1)
                dve.memset(ones[:], 1.0)
                dve.wait_ge(many_ok, 1)
                dve.tensor_scalar(many[:, 0:1], most[:], float(EXACT), None, ALU.is_gt)
                dve.tensor_scalar(many[:, 1:2], most[:], float(EXACT), None, ALU.is_gt).then_inc(many_ok, 1)
                dve.wait_ge(many_mm, 1)
                dve.tensor_copy(many_i[:], sum_bank[0][0:1, 0:2]).then_inc(many_read, 1)
            pairs(dve, mix)

    @block.scalar
    def _(act):
        def copy_h(q, n, u):
            g = NB * q + n
            if q:
                act.wait_ge(h_ok, NB * (q - 1) + n + 1)
            need(act, turned, g - 1)
            act.activation(hc[u][:], tile_of(h, n), ACT.Copy).then_inc(hc_ok, 1)

        def convert(q, n, u):
            need(act, sum_mm, NB * q + n - 1)
            act.activation(a_hi[u][:], tile_of(k["adj"], n)[0:NPB, :], ACT.Copy).then_inc(a_hi_ok, 1)

        def high(g, u):
            act.wait_ge(turned, g + 1)
            need(act, prod_mm, g - 1)
            act.activation(ht_hi[u][:, :, 0:NPB], spread(turn_bank[u]), ACT.Copy).then_inc(ht_hi_ok, 1)

        copy_h(0, 0, 0)
        act.activation(w_hi[0][:], w[0][:], ACT.Copy).then_inc(w_hi_ok, 1)
        high(0, 0)
        copy_h(0, 1, 1)
        act.activation(w_hi[1][:], w[1][:], ACT.Copy).then_inc(w_hi_ok, 1)
        for q in range(PASSES):
            def evacuate(i, q=q):
                for u in range(2):
                    n = 2 * i + u
                    g = NB * q + n
                    if not (isinstance(n, int) and n == NB - 1):
                        high(g + 1, 1 - u)
                    if not (isinstance(n, int) and n >= NB - 2):
                        copy_h(q, n + 2, u)
                    if q < LAYERS:
                        act.wait_ge(prod_mm, g + 1)
                        act.activation(tile_of(u_hi, n), neigh_bank[u][0:NPB, :], ACT.Copy).then_inc(u_hi_ok, 1)

            pairs(act, evacuate)
            if q == LAYERS:
                break

            def rectify(i, q=q):
                for u in range(2):
                    n = 2 * i + u
                    g = NB * q + n
                    if not (isinstance(n, int) and n == NB - 1):
                        convert(q, n + 1, 1 - u)
                    else:
                        copy_h(q + 1, 0, 0)
                        copy_h(q + 1, 1, 1)
                        high(g + 1, 0)
                    if q < LAYERS - 1:
                        act.wait_ge(mixed_ok, g + 1)
                        act.activation(tile_of(h, n), mixed[u][:], ACT.Relu).then_inc(h_ok, 1)

            if q == 0:
                act.wait_ge(counts_ok, NB - 1)
            convert(q, 0, 0)
            pairs(act, rectify)

    @block.tensor
    def _(pe):
        def turn(g, u):
            pe.wait_ge(hc_ok, g + 1)
            need(pe, ht_lo_ok, g - 1)
            for c in range(KC):
                last = pe.transpose(turn_bank[u][:, c * P:c * P + NPB], hc[u][:, c * P:(c + 1) * P], k["ident"][0:NPB, 0:NPB])
            last.then_inc(turned, 1)

        for q in range(PASSES):
            def multiply(i, q=q):
                for u in range(2):
                    n = 2 * i + u
                    g = NB * q + n
                    if not (isinstance(n, int) and n == NB - 1):
                        turn(g + 1, 1 - u)
                    pe.wait_ge(ht_lo_ok, g + 1)
                    if q < LAYERS:
                        need(pe, self_ok, g - 1)
                    need(pe, u_lo_ok, g - 1)
                    left = (lambda c: ht_hi[u][:, c, 0:NPB], lambda c: ht_lo[u][:, c, 0:NPB])
                    for b, j in ((self_bank, 0), (neigh_bank, 1)):
                        if q == 0 and isinstance(n, int) and n == 0 and j == 1:
                            pe.wait_ge(w_split, 1)
                        last = product(pe, b[u][0:NPB, :], left, (lambda c: w_hi[j][:, c, :], lambda c: w_lo[j][:, c, :]), range(KC))
                    last.then_inc(prod_mm, 1)

            if q == 0:
                turn(0, 0)
            if q:
                pe.wait_ge(w_split, q + 1)
            else:
                pe.wait_ge(self_split, 1)
            pairs(pe, multiply)
            if q == LAYERS:
                break
            pe.wait_ge(u_lo_ok, NB * (q + 1))

            if q == 0:
                pe.wait_ge(many_ok, 2)
                pe.matmul(sum_bank[0][0:1, 0:2], many[:, 0:1], ones[:], start=True, stop=True).then_inc(many_mm, 1)
                pe.wait_ge(many_read, 1)
                inexact = pe.value_load(many_i[0:1, 0:1], min_val=0, max_val=P)

            def add_up(i, q=q):
                for u in range(2):
                    g = NB * q + 2 * i + u
                    if isinstance(i, int) and i and u:
                        turn(g + 1, 0)
                    pe.wait_ge(a_lo_ok, g + 1)
                    need(pe, mixed_ok, g - 1)
                    for s in range(NB):
                        high = a_hi[u][:, s * P:(s + 1) * P]
                        pe.matmul(sum_bank[u][:], high, u_hi[:, s, :], start=(s == 0), stop=False, skip_group_check=True)
                        if s == 0:
                            with pe.If(inexact > 0):
                                for c in range(NB):
                                    pe.matmul(sum_bank[u][:], a_lo[u][:, c * P:(c + 1) * P], u_hi[:, c, :], start=False,
                                              stop=False, skip_group_check=True)
                        last = pe.matmul(sum_bank[u][:], high, u_lo[:, s, :], start=False, stop=(s == NB - 1), skip_group_check=True)
                    last.then_inc(sum_mm, 1)

            pairs(pe, add_up)


def phase_c(nc, ctx, t, scratch, keep):
    def sb(name, shape, dt=F32):
        return ctx.enter_context(nc.sbuf_tensor("c_" + name, shape, dt))

    def sem(name):
        return ctx.enter_context(nc.semaphore("c_" + name))

    def psum(name):
        return ctx.enter_context(nc.psum_tensor("c_" + name, [P, 512], F32))

    feat_bank, var1_bank, edge_bank, turn_bank, var2_bank = (
        psum(n) for n in ("feat_bank", "var1_bank", "edge_bank", "turn_bank", "var2_bank"))
    sum_p_bank, sum_h_bank, sum_r_bank = psum("sum_p_bank"), psum("sum_h_bank"), psum("sum_r_bank")
    mats = ("square1", "fold_edge", "square2")
    biases = ("lin1", "fold_edge_b", "lin2")
    m_hi = [sb(f"m_hi{i}", [P, KC, D], F32R) for i in range(3)]
    m_lo = [sb(f"m_lo{i}", [P, KC, D], F32R) for i in range(3)]
    bias = sb("bias", [P, 3, D])
    w0 = sb("w0", [P, D], F32R)
    zeros16 = sb("zeros16", [P, 512], BF16)
    attr_hi = sb("attr_hi", [P, GROUP, A4], F32R)
    stack = sb("stack", [P, GROUP, STK])
    attr_t = sb("attr_t", [P, P], F32R)
    at_nodes = [sb(f"at_nodes{i}", [P, 2], I32) for i in range(4)]
    node_at = sb("node_at", [P, TILES, 2], I32)
    dst_in = sb("dst_in", [P, TILES])
    from_src = [sb(f"from_src{i}", [P, D]) for i in range(4)]
    from_dst = [sb(f"from_dst{i}", [P, D]) for i in range(4)]
    pt_f = [sb(f"pt_f{i}", [P, KC, P]) for i in range(2)]
    pt_hi = [sb(f"pt_hi{i}", [P, KC, P], F32R) for i in range(2)]
    pt_lo = [sb(f"pt_lo{i}", [P, KC, P], F32R) for i in range(2)]
    p = [sb(f"p{i}", [P, D]) for i in range(2)]
    hot = [sb(f"hot{i}", [P, P], F32R) for i in range(4)]
    var = [sb(f"var{i}", [P, 4]) for i in range(4)]
    dev = [sb(f"dev{i}", [P, 4]) for i in range(4)]
    dev_parts = [sb(f"dev_parts{i}", [P, 8], F32R) for i in range(4)]
    with ExitStack() as early:
        def sb_early(name, shape, dt=F32):
            return early.enter_context(nc.sbuf_tensor("c_" + name, shape, dt))

        staging = [sb_early(f"staging{i}", [P, KC, D]) for i in range(3)]
        w0_f, w0_hi, w0_lo = sb_early("w0_f", [A4 + 1, D]), sb_early("w0_hi", [A4 + 1, D], F32R), sb_early("w0_lo", [A4 + 1, D], F32R)
    h = [sb(f"h{i}", [P, D]) for i in range(2)]
    ht_hi = [sb(f"ht_hi{i}", [P, KC, P], F32R) for i in range(2)]
    ht_lo = [sb(f"ht_lo{i}", [P, KC, P], F32R) for i in range(2)]
    rp_hi = [sb(f"rp_hi{i}", [P, D], F32R) for i in range(4)]
    rp_lo = [sb(f"rp_lo{i}", [P, D], F32R) for i in range(4)]
    rh_hi = [sb(f"rh_hi{i}", [P, D], F32R) for i in range(2)]
    rh_lo = [sb(f"rh_lo{i}", [P, D], F32R) for i in range(2)]
    k = keep

    mat_in = [sem(f"mat_in{i}") for i in range(3)]
    small_in, split_ok, mat_hi_ok = sem("small_in"), sem("split_ok"), sem("mat_hi_ok")
    opened, next_in = sem("opened"), sem("next_in")
    parts_hi_ok, parts_ok = sem("parts_hi_ok"), sem("parts_ok")
    rows_split, placed, set_up, tick, w0_zero = sem("rows_split"), sem("placed"), sem("set_up"), sem("tick"), sem("w0_zero")
    attr_hi_ok, stack_ok, stack_turned, attr_t_ok = (sem(n) for n in ("attr_hi_ok", "stack_ok", "stack_turned", "attr_t_ok"))
    pt_mm, p_mm, pt_hi_ok, pt_f_ok, p_ok, pt_lo_ok = (sem(n) for n in ("pt_mm", "p_mm", "pt_hi_ok", "pt_f_ok", "p_ok", "pt_lo_ok"))
    var1_mm, var1_ok, bound1_ok, dev1_ok = (sem(n) for n in ("var1_mm", "var1_ok", "bound1_ok", "dev1_ok"))
    at_ok, added_ok, edge_mm, z_ok, h_ok = (sem(n) for n in ("at_ok", "added_ok", "edge_mm", "z_ok", "h_ok"))
    bias_in = sem("bias_in")
    var1_set, edge_set, var2_set = sem("var1_set"), sem("edge_set"), sem("var2_set")
    src_in = [sem(f"src_in{i}") for i in range(4)]
    dst_rows_in = [sem(f"dst_in{i}") for i in range(4)]
    h_turned, ht_hi_ok, ht_lo_ok = sem("h_turned"), sem("ht_hi_ok"), sem("ht_lo_ok")
    var2_mm, var2_ok, bound2_ok, dev2_ok = (sem(n) for n in ("var2_mm", "var2_ok", "bound2_ok", "dev2_ok"))
    rp_hi_ok, rp_lo_ok, rh_hi_ok, rh_lo_ok, hot_ok = (sem(n) for n in ("rp_hi_ok", "rp_lo_ok", "rh_hi_ok", "rh_lo_ok", "hot_ok"))
    sums_mm, sums_read, sums_left = sem("sums_mm"), sem("sums_read"), sem("sums_left")

    def steps(engine, step):
        for u in range(GROUP):
            step(0, u)
        with engine.Fori(1, GROUPS - 1) as i:
            for u in range(GROUP):
                step(i, u)
        for u in range(GROUP):
            step(GROUPS - 1, u)

    def at(tensor, n, width=1):
        return tensor[:, n:n + width] if isinstance(n, int) else tensor[:, ds(n, width)]

    def exists(n):
        return not isinstance(n, int) or 0 <= n < TILES

    block = ctx.enter_context(nc.Block())

    @block.sync
    def _(sp):
        sp.dma_start(w0_f[0:A4, :], t["L1_gnn_emb_W0"]).then_inc(small_in, 16)
        sp.dma_start(w0_f[A4:A4 + 1, :], rows(t["L1_gnn_emb_b0"])).then_inc(small_in, 16)
        sp.dma_start(staging[0][:], chunked(scratch[mats[0]])).then_inc(mat_in[0], 16)
        sp.wait_ge(placed, 16 * 3 * GROUP)
        for i, name in enumerate(biases):
            sp.dma_start(bias[:, i, :], rows(scratch[name]).broadcast_to([P, D])).then_inc(bias_in, 16)
            if i:
                sp.dma_start(staging[i][:], chunked(scratch[mats[i]])).then_inc(mat_in[i], 16)
        sp.wait_ge(split_ok, 3)
        for i, m in enumerate((scratch["fold_node1"], scratch["fold_node2"], t["L1_gnn_node_W1"])):
            sp.dma_start(k[f"node_mat{i}"][:], chunked(m)).then_inc(next_in, 16)
        sp.wait_ge(next_in, 48)

    @block.gpsimd
    def _(pool):
        def build_stack(g):
            rec = k["recs"][:, g * GROUP:(g + 1) * GROUP, :] if isinstance(g, int) else k["recs"][:, ds(g * GROUP, GROUP), :]
            attr = rec[:, :, F_ATTR:F_ATTR + A4]
            if not isinstance(g, int) or g:
                pool.wait_ge(stack_turned, g)
                pool.sem_inc(tick, 1)
            pool.tensor_copy(attr_hi[:], attr).then_inc(attr_hi_ok, 1)
            pool.wait_ge(attr_hi_ok, g + 1)
            pool.sem_inc(tick, 1)
            pool.tensor_copy(stack[:, :, 0:A4], attr_hi[:].bitcast(F32))
            pool.tensor_copy(stack[:, :, 5:5 + A4], attr_hi[:].bitcast(F32))
            pool.tensor_tensor(stack[:, :, 10:10 + A4], attr, attr_hi[:].bitcast(F32), ALU.subtract).then_inc(stack_ok, 1)

        def gather(n, u):
            if not isinstance(n, int) or n >= 4:
                pool.wait_ge(h_ok, n - 3)
                pool.sem_inc(tick, 1)
            pool.tensor_copy(at_nodes[u][:], node_at[:, n, :] if isinstance(n, int)
                             else node_at[:, ds(n, 1), :].rearrange("p a b -> p (a b)")).then_inc(at_ok, 1)
            pool.wait_ge(at_ok, n + 1)
            pool.sem_inc(tick, 1)
            pool.indirect_dma_start(from_src[u][:], None, scratch["mesh_table"],
                                    bass.IndirectOffsetOnAxis(ap=at_nodes[u][:, 0:1], axis=0)).then_inc(src_in[u], 16)
            pool.indirect_dma_start(from_dst[u][:], None, scratch["dst_table"],
                                    bass.IndirectOffsetOnAxis(ap=at_nodes[u][:, 1:2], axis=0)).then_inc(dst_rows_in[u], 16)

        def add(n, u):
            pool.wait_ge(src_in[u], (n - u) * 4 + 16)
            pool.wait_ge(dst_rows_in[u], (n - u) * 4 + 16)
            pool.sem_inc(tick, 1)
            pool.tensor_tensor(from_src[u][:], from_src[u][:], from_dst[u][:], ALU.add).then_inc(added_ok, 1)

        def deviation2(n, u):
            pool.wait_ge(bound2_ok, n + 1)
            pool.tensor_tensor(dev[u][:, 1:2], var[u][:, 3:4], k["half"][:], ALU.pow).then_inc(dev2_ok, 1)
            pool.wait_ge(dev2_ok, n + 1)
            pool.sem_inc(tick, 1)
            if not isinstance(n, int) or n >= 4:
                pool.wait_ge(sums_mm, n - 3)
                pool.sem_inc(tick, 1)
            pool.tensor_copy(dev_parts[u][:, 0:4], dev[u][:]).then_inc(parts_hi_ok, 1)
            pool.wait_ge(parts_hi_ok, n + 1)
            pool.sem_inc(tick, 1)
            pool.tensor_tensor(dev_parts[u][:, 4:8], dev[u][:], dev_parts[u][:, 0:4].bitcast(F32), ALU.subtract).then_inc(parts_ok, 1)

        def step(i, u):
            n = GROUP * i + u
            if exists(n + 3):
                gather(n + 3, (u + 3) % 4)
            if u == 0 and exists(n + GROUP):
                build_stack(i + 1)
            pool.wait_ge(bound1_ok, n + 1)
            pool.tensor_tensor(dev[u][:, 0:1], var[u][:, 2:3], k["half"][:], ALU.pow).then_inc(dev1_ok, 1)
            if exists(n + 1):
                add(n + 1, (u + 1) % 4)
            if exists(n - 1):
                deviation2(n - 1, (u - 1) % 4)

        pool.wait_ge(set_up, 1)
        build_stack(0)
        for u in range(3):
            gather(u, u)
        add(0, 0)
        steps(pool, step)
        deviation2(TILES - 1, 3)

    @block.vector
    def _(dve):
        dve.memset(stack[:], 0.0)
        dve.tensor_copy(node_at[:, :, 0], k["recs"][:, :, F_SRC])
        dve.tensor_copy(node_at[:, :, 1], k["recs"][:, :, F_DSTG])
        dve.tensor_copy(dst_in[:], k["recs"][:, :, F_DST])
        for u in range(4):
            dve.memset(dev[u][:, 2:3], 1.0)
            dve.memset(dev[u][:, 3:4], 0.0)
        dve.memset(zeros16[:], 0.0)
        dve.memset(w0[:].bitcast(F32), 0.0).then_inc(w0_zero, 1)
        dve.wait_ge(w0_zero, 1)
        dve.memset(stack[:, :, A4:A4 + 1], 1.0)
        dve.memset(stack[:, :, 2 * A4 + 1:2 * A4 + 2], 1.0).then_inc(set_up, 1)
        dve.wait_ge(rows_split, 1)
        dve.tensor_tensor(w0_lo[:], w0_f[:], w0_hi[:].bitcast(F32), ALU.subtract).then_inc(rows_split, 1)

        def split(i):
            dve.wait_ge(mat_hi_ok, i + 1)
            dve.tensor_tensor(m_lo[i][:], staging[i][:], m_hi[i][:].bitcast(F32), ALU.subtract).then_inc(split_ok, 1)

        def low_p(n, u):
            dve.wait_ge(pt_f_ok, n + 1)
            need(dve, edge_mm, n - 1)
            dve.tensor_tensor(pt_lo[u % 2][:], pt_f[u % 2][:], pt_hi[u % 2][:].bitcast(F32), ALU.subtract).then_inc(pt_lo_ok, 1)

        def low_rh(n, u):
            dve.wait_ge(rh_hi_ok, n + 1)
            need(dve, sums_mm, n - 1)
            dve.scalar_tensor_tensor(out=rh_lo[u % 2][:], in0=h[u % 2][:], scalar=dev[u][:, 1:2], in1=rh_hi[u % 2][:].bitcast(F32),
                                     op0=ALU.mult, op1=ALU.subtract).then_inc(rh_lo_ok, 1)
            dve.tensor_scalar(hot[u][:], k["grid"][:], at(dst_in, n), None, ALU.is_equal).then_inc(hot_ok, 1)

        def leave(n):
            last = dve.value_load(at(k["tile_last"][0:1, :], n), min_val=0, max_val=NB)
            with dve.If(last > 0):
                b = nc.s_assert_within(last - 1, 0, NB - 1)
                dve.wait_ge(sums_mm, n + 1)
                dve.sem_inc(tick, 1)
                dve.tensor_copy(tile_of(k["sum_p"], b), sum_p_bank[:])
                dve.tensor_copy(tile_of(k["sum_h"], b), sum_h_bank[:])
                dve.tensor_copy(tile_of(k["sum_r"], b), sum_r_bank[:, 0:8]).then_inc(sums_read, 1)
                dve.wait_ge(sums_read, last)
                dve.memset(sum_p_bank[:], 0.0)
                dve.memset(sum_h_bank[:], 0.0)
                dve.memset(sum_r_bank[:, 0:8], 0.0).then_inc(sums_left, 1)

        def variance2(n, u):
            dve.wait_ge(var2_mm, n + 1)
            dve.tensor_tensor_reduce(var2_bank[:], var2_bank[:], h[u % 2][:], 1.0 / D, k["floor"][:, 1:2],
                                     ALU.mult, ALU.add, var[u][:, 1:2]).then_inc(var2_ok, 1)
            dve.wait_ge(var2_ok, n + 1)
            dve.tensor_scalar(var[u][:, 3:4], var[u][:, 1:2], EPS, None, ALU.max).then_inc(bound2_ok, 1)

        def low_ht(n, u):
            dve.wait_ge(ht_hi_ok, n + 1)
            need(dve, var2_mm, n - 1)
            dve.tensor_tensor(ht_lo[u % 2][:], turn_bank[:].rearrange("p (k n) -> p k n", k=KC), ht_hi[u % 2][:].bitcast(F32),
                              ALU.subtract).then_inc(ht_lo_ok, 1)

        def step(i, u):
            n = GROUP * i + u
            dve.wait_ge(var1_mm, n + 1)
            dve.wait_ge(p_ok, n + 1)
            dve.tensor_tensor_reduce(var1_bank[:], var1_bank[:], p[u % 2][:], 1.0 / D, k["floor"][:, 0:1],
                                     ALU.mult, ALU.add, var[u][:, 0:1]).then_inc(var1_ok, 1)
            dve.wait_ge(var1_ok, n + 1)
            dve.tensor_scalar(var[u][:, 2:3], var[u][:, 0:1], EPS, None, ALU.max).then_inc(bound1_ok, 1)
            if exists(n - 2):
                low_rh(n - 2, (u - 2) % 4)
            if exists(n + 1):
                low_p(n + 1, (u + 1) % 4)
            if exists(n - 1):
                low_ht(n - 1, (u - 1) % 4)
            if exists(n - 3):
                leave(n - 3)
            dve.wait_ge(rp_hi_ok, n + 1)
            dve.scalar_tensor_tensor(out=rp_lo[u][:], in0=p[u % 2][:], scalar=dev[u][:, 0:1], in1=rp_hi[u][:].bitcast(F32),
                                     op0=ALU.mult, op1=ALU.subtract).then_inc(rp_lo_ok, 1)
            dve.wait_ge(edge_mm, n + 1)
            dve.wait_ge(added_ok, n + 1)
            dve.scalar_tensor_tensor(out=from_src[u][:], in0=edge_bank[:], scalar=dev[u][:, 0:1], in1=from_src[u][:],
                                     op0=ALU.mult, op1=ALU.add).then_inc(z_ok, 1)
            if exists(n - 1):
                variance2(n - 1, (u - 1) % 4)

        split(0)
        low_p(0, 0)
        split(1)
        split(2)
        steps(dve, step)
        last = TILES - 1
        low_ht(last, 3)
        leave(last - 2)
        low_rh(last - 1, 2)
        variance2(last, 3)
        leave(last - 1)
        low_rh(last, 3)
        leave(last)

    @block.scalar
    def _(act):
        act.wait_ge(small_in, 32)
        act.activation(w0_hi[:], w0_f[:], ACT.Copy).then_inc(rows_split, 1)
        act.wait_ge(rows_split, 2)
        act.wait_ge(w0_zero, 1)
        for j in range(GROUP):
            base = STK * j
            act.dma_start(w0[base:base + 5, :].bitcast(F32), w0_hi[:].bitcast(F32)).then_inc(placed, 16)
            act.dma_start(w0[base + 5:base + 10, :].bitcast(F32), w0_lo[:].bitcast(F32)).then_inc(placed, 16)
            act.dma_start(w0[base + 10:base + 14, :].bitcast(F32), w0_hi[0:A4, :].bitcast(F32)).then_inc(placed, 16)

        def turn_out(g):
            act.wait_ge(stack_turned, g + 1)
            act.activation(attr_t[:], turn_bank[:, 0:P], ACT.Copy).then_inc(attr_t_ok, 1)

        def hidden(n, u):
            act.wait_ge(pt_mm, n + 1)
            need(act, pt_lo_ok, n - 1)
            need(act, edge_mm, n - 1)
            act.activation(pt_hi[u % 2][:], feat_bank[:].rearrange("p (k n) -> p k n", k=KC), ACT.Silu).then_inc(pt_hi_ok, 1)
            act.activation(pt_f[u % 2][:], feat_bank[:].rearrange("p (k n) -> p k n", k=KC), ACT.Silu).then_inc(pt_f_ok, 1)

        def hidden_rows(n, u):
            act.wait_ge(p_mm, n + 1)
            need(act, rp_lo_ok, n - 1)
            act.activation(p[u % 2][:], feat_bank[:], ACT.Silu).then_inc(p_ok, 1)

        def high_rh(n, u):
            act.wait_ge(dev2_ok, n + 1)
            need(act, sums_mm, n - 1)
            act.activation(rh_hi[u % 2][:], h[u % 2][:], ACT.Copy, scale=dev[u][:, 1:2]).then_inc(rh_hi_ok, 1)

        def high_ht(n, u):
            act.wait_ge(h_turned, n + 1)
            need(act, var2_mm, n - 1)
            act.activation(ht_hi[u % 2][:], turn_bank[:].rearrange("p (k n) -> p k n", k=KC), ACT.Copy).then_inc(ht_hi_ok, 1)

        def bias_into(bank, m, bank_set):
            act.activation(bank[:], bias[:, m, :], ACT.Copy).then_inc(bank_set, 1)

        def step(i, u):
            n = GROUP * i + u
            if u == GROUP - 1 and exists(n + 1):
                turn_out(i + 1)
            if exists(n + 1):
                hidden(n + 1, (u + 1) % 4)
            if exists(n - 1):
                need(act, var2_ok, n - 1)
                bias_into(var2_bank, 2, var2_set)
            if exists(n - 2):
                high_rh(n - 2, (u - 2) % 4)
            if exists(n + 1):
                hidden_rows(n + 1, (u + 1) % 4)
            if exists(n - 1):
                high_ht(n - 1, (u - 1) % 4)
            if exists(n + 1):
                act.wait_ge(var1_ok, n + 1)
                bias_into(var1_bank, 0, var1_set)
            act.wait_ge(dev1_ok, n + 1)
            need(act, sums_mm, n - 3)
            act.activation(rp_hi[u][:], p[u % 2][:], ACT.Copy, scale=dev[u][:, 0:1]).then_inc(rp_hi_ok, 1)
            act.wait_ge(z_ok, n + 1)
            need(act, rh_lo_ok, n - 1)
            need(act, h_turned, n - 1)
            act.activation(h[u % 2][:], from_src[u][:], ACT.Silu).then_inc(h_ok, 1)
            if exists(n + 1):
                bias_into(edge_bank, 1, edge_set)

        def matrix(i):
            act.wait_ge(mat_in[i], 16)
            act.activation(m_hi[i][:], staging[i][:], ACT.Copy).then_inc(mat_hi_ok, 1)

        matrix(0)
        turn_out(0)
        hidden(0, 0)
        hidden_rows(0, 0)
        matrix(1)
        act.wait_ge(bias_in, 48)
        act.wait_ge(opened, 1)
        bias_into(var1_bank, 0, var1_set)
        bias_into(edge_bank, 1, edge_set)
        matrix(2)
        steps(act, step)
        last = TILES - 1
        act.wait_ge(var2_ok, last)
        bias_into(var2_bank, 2, var2_set)
        high_ht(last, 3)
        high_rh(last - 1, 2)
        high_rh(last, 3)

    @block.tensor
    def _(pe):
        def turn_stack(g):
            pe.wait_ge(stack_ok, g + 1)
            pe.transpose(turn_bank[:, 0:P], stack[:].rearrange("p t f -> p (t f)"), k["ident"][:]).then_inc(stack_turned, 1)

        def features(n, u):
            need(pe, p_ok, n)
            part = slice(STK * u, STK * (u + 1))
            for c in range(KC):
                last = pe.matmul(feat_bank[:, c * P:(c + 1) * P], w0[part, c * P:(c + 1) * P], attr_t[part, :],
                                 start=True, stop=True, skip_group_check=True)
            last.then_inc(pt_mm, 1)

        def feature_rows(n, u):
            pe.wait_ge(pt_f_ok, n + 1)
            part = slice(STK * u, STK * (u + 1))
            pe.matmul(feat_bank[:], attr_t[part, :], w0[part, :], start=True, stop=True).then_inc(p_mm, 1)

        def square(out, left, m):
            for c in range(KC):
                part = SQUARE_BLOCKS[c]
                to, high, low = (b.rearrange("p (k n) -> p k n", k=KC)[:, part, :] for b in (out[:], m_hi[m][:, c, :], m_lo[m][:, c, :]))
                pe.matmul(to, left[0][:, c, :], high, start=False, stop=False, skip_group_check=True)
                pe.matmul(to, left[0][:, c, :], low, start=False, stop=False, skip_group_check=True)
                last = pe.matmul(to, left[1][:, c, :], high, start=False, stop=(c == KC - 1), skip_group_check=True)
            return last

        def turn_h(n, u):
            pe.wait_ge(h_ok, n + 1)
            need(pe, ht_lo_ok, n)
            for c in range(KC):
                last = pe.transpose(turn_bank[:, c * P:(c + 1) * P], h[u % 2][:, c * P:(c + 1) * P], k["ident"][:])
            last.then_inc(h_turned, 1)

        def variance2(n, u):
            if isinstance(n, int) and n == 0:
                pe.wait_ge(split_ok, 3)
            pe.wait_ge(ht_lo_ok, n + 1)
            pe.wait_ge(var2_set, n + 1)
            square(var2_bank, (ht_hi[u % 2], ht_lo[u % 2]), 2).then_inc(var2_mm, 1)

        def sums(n, u):
            pe.wait_ge(rp_lo_ok, n + 1)
            pe.wait_ge(hot_ok, n + 1)
            pe.wait_ge(parts_ok, n + 1)
            pe.wait_ge(sums_left, pe.value_load(at(k["tile_bucket1"][0:1, :], n), min_val=1, max_val=NB))
            for bank, part in ((sum_p_bank, rp_hi[u]), (sum_p_bank, rp_lo[u]), (sum_h_bank, rh_hi[u % 2]), (sum_h_bank, rh_lo[u % 2])):
                pe.matmul(bank[:], hot[u][:], part[:], start=False, stop=False, skip_group_check=True)
            pe.matmul(sum_r_bank[:, 0:8], hot[u][:], dev_parts[u][:], start=False, stop=False,
                      skip_group_check=True).then_inc(sums_mm, 1)

        def step(i, u):
            n = GROUP * i + u
            if u == GROUP - 1 and exists(n + 1):
                pe.wait_ge(attr_t_ok, i + 2)
            if exists(n + 1):
                features(n + 1, (u + 1) % 4)
            if isinstance(n, int) and n == 0:
                pe.wait_ge(split_ok, 1)
            pe.wait_ge(pt_lo_ok, n + 1)
            pe.wait_ge(var1_set, n + 1)
            square(var1_bank, (pt_hi[u % 2], pt_lo[u % 2]), 0).then_inc(var1_mm, 1)
            if exists(n + 1):
                feature_rows(n + 1, (u + 1) % 4)
            if exists(n - 1):
                turn_h(n - 1, (u - 1) % 4)
            pe.wait_ge(edge_set, n + 1)
            if isinstance(n, int) and n == 0:
                pe.wait_ge(split_ok, 2)
            for c in range(KC):
                left = (pt_hi[u % 2][:, c, :], pt_lo[u % 2][:, c, :])
                pe.matmul(edge_bank[:], left[0], m_hi[1][:, c, :], start=False, stop=False, skip_group_check=True)
                pe.matmul(edge_bank[:], left[0], m_lo[1][:, c, :], start=False, stop=False, skip_group_check=True)
                last = pe.matmul(edge_bank[:], left[1], m_hi[1][:, c, :], start=False, stop=(c == KC - 1), skip_group_check=True)
            last.then_inc(edge_mm, 1)
            if exists(n - 1):
                variance2(n - 1, (u - 1) % 4)
            if u == GROUP - 2 and exists(n + 2):
                turn_stack(i + 1)
            if exists(n - 2):
                sums(n - 2, (u - 2) % 4)

        pe.wait_ge(set_up, 1)
        for bank in (sum_p_bank, sum_h_bank, sum_r_bank, var1_bank, edge_bank, var2_bank):
            last = pe.matmul(bank[:], zeros16[:, 0:P], zeros16[:], start=True, stop=False, skip_group_check=True)
        last.then_inc(opened, 1)
        pe.sem_inc(sums_left, 1)
        pe.wait_ge(placed, 16 * 3 * GROUP)
        turn_stack(0)
        pe.wait_ge(attr_t_ok, 1)
        features(0, 0)
        feature_rows(0, 0)
        steps(pe, step)
        last = TILES - 1
        turn_h(last, 3)
        sums(last - 1, 2)
        variance2(last, 3)
        sums(last, 3)


def phase_d(nc, ctx, t, scratch, keep, out_dram):
    def sb(name, shape, dt=F32):
        return ctx.enter_context(nc.sbuf_tensor("d_" + name, shape, dt))

    def sem(name):
        return ctx.enter_context(nc.semaphore("d_" + name))

    def psum(name):
        return ctx.enter_context(nc.psum_tensor("d_" + name, [P, 512], F32))

    turn_bank = [psum(f"turn_bank{i}") for i in range(2)]
    small_bank, hidden_bank, hturn_bank, node_bank = (psum(n) for n in ("small_bank", "hidden_bank", "hturn_bank", "node_bank"))
    m_f = [keep[f"node_mat{i}"] for i in range(3)]
    m_hi = [sb(f"m_hi{i}", [P, KC, D], F32R) for i in range(3)]
    m_lo = [sb(f"m_lo{i}", [P, KC, D], F32R) for i in range(3)]
    row_fold = sb("row_fold", [8, D])
    b1, gain, shift = (sb(n, [NPB, D]) for n in ("b1", "gain", "shift"))
    s_in = [[sb(f"s_in{j}{i}", [NPB, D]) for i in range(2)] for j in range(2)]
    r_in = [sb(f"r_in{i}", [NPB, 8]) for i in range(2)]
    s_hi = [sb(f"s_hi{j}", [P, KC, P], F32R) for j in range(2)]
    s_lo = [sb(f"s_lo{j}", [P, KC, P], F32R) for j in range(2)]
    r_t = sb("r_t", [8, NPB])
    own = [sb(f"own{i}", [NPB, D]) for i in range(2)]
    added = [sb(f"added{i}", [NPB, D]) for i in range(2)]
    x1 = [sb(f"x1{i}", [NPB, D]) for i in range(2)]
    x2 = [sb(f"x2{i}", [NPB, D]) for i in range(2)]
    hidden = [sb(f"hidden{i}", [NPB, D]) for i in range(2)]
    y, final = sb("y", [NPB, D]), [sb(f"final{i}", [NPB, D]) for i in range(2)]
    nt_hi, nt_lo = sb("nt_hi", [P, KC, P], F32R), sb("nt_lo", [P, KC, P], F32R)
    stats, moments, dev = (sb(n, [NPB, 8]) for n in ("stats", "moments", "dev"))
    k = keep

    x1_in, x2_ok, doubled = [sem(f"x1_in{i}") for i in range(2)], sem("x2_ok"), sem("doubled")
    row_in, mat_ok, mat_hi_ok, tick, zeroed = (sem(n) for n in ("row_in", "mat_ok", "mat_hi_ok", "tick", "zeroed"))
    tile_in = [sem(f"tile_in{i}") for i in range(2)]
    stored = [sem(f"stored{i}") for i in range(2)]
    copied, turned, r_turned, s_hi_ok, s_lo_ok, r_t_ok = (
        sem(n) for n in ("copied", "turned", "r_turned", "s_hi_ok", "s_lo_ok", "r_t_ok"))
    hidden_mm, own_ok, hidden_ok, hidden_turned, nt_hi_ok, nt_lo_ok, node_mm = (
        sem(n) for n in ("hidden_mm", "own_ok", "hidden_ok", "hidden_turned", "nt_hi_ok", "nt_lo_ok", "node_mm"))
    y_step, var_ok, dev_ok, final_ok = (sem(n) for n in ("y_step", "var_ok", "dev_ok", "final_ok"))
    STEPS = 7

    def spread(b):
        return b[:].rearrange("p (k n) -> p k n", k=KC)[:, :, 0:NPB]

    def exists(n):
        return not isinstance(n, int) or n >= 0

    block = ctx.enter_context(nc.Block())

    @block.sync
    def _(sp):
        sp.wait_ge(zeroed, 1)
        for j, name in enumerate(("node_r1", "node_r2", "node_count")):
            for part in range(2):
                sp.dma_start(row_fold[4 * part + j:4 * part + j + 1, :], rows(scratch[name])).then_inc(row_in, 16)
        for to, name in ((shift, "node_beta"), (b1, "node_b1"), (gain, "node_g")):
            sp.dma_start(to[:], rows(t["L1_gnn_" + name]).broadcast_to([NPB, D])).then_inc(row_in, 16)

        def tiles(i):
            for u in range(2):
                n = 2 * i + u
                need(sp, own_ok, n - 1)
                sp.dma_start(own[u][:], node_rows(scratch["node_own"], n)).then_inc(tile_in[u], 16)
                need(sp, x2_ok, n - 1)
                sp.dma_start(x1[u][:], node_rows(scratch["x1"], n)).then_inc(x1_in[u], 16)
            for u in range(2):
                n = 2 * i + u - 2
                if not isinstance(n, int) or n >= 0:
                    store(n, u)

        def store(n, u):
            sp.wait_ge(final_ok, n + 1)
            sp.dma_start(node_rows(out_dram, n), final[u][:]).then_inc(stored[u], 16)

        pairs(sp, tiles)
        for u in range(2):
            store(NB - 2 + u, u)
        for u in range(2):
            sp.wait_ge(stored[u], 16 * NB // 2)

    @block.gpsimd
    def _(pool):
        pool.memset(row_fold[:], 0.0).then_inc(zeroed, 1)
        pool.wait_ge(row_in, 144)

        def double(n, u):
            need(pool, final_ok, n - 1)
            pool.wait_ge(x1_in[u], (n - u) * 8 + 16)
            pool.sem_inc(tick, 1)
            pool.tensor_tensor(x2[u][:], x1[u][:], x1[u][:], ALU.add).then_inc(doubled, 1)
            pool.wait_ge(doubled, n + 1)
            pool.sem_inc(tick, 1)
            pool.tensor_tensor(x2[u][:], x2[u][:], shift[:], ALU.add).then_inc(x2_ok, 1)

        def tiles(i):
            for u in range(2):
                double(2 * i + u, u)
            for u in range(2):
                for norm in range(2):
                    m = 2 * (2 * i + u) + norm
                    pool.wait_ge(var_ok, m + 1)
                    pool.tensor_tensor(dev[:, 1:2], dev[:, 0:1], k["half"][0:NPB, :], ALU.pow).then_inc(dev_ok, 1)

        pairs(pool, tiles)

    @block.vector
    def _(dve):
        def low_sums(n):
            need(dve, hidden_mm, n)
            dve.wait_ge(r_turned, n + 1)
            dve.tensor_copy(r_t[:], small_bank[0:8, 0:NPB]).then_inc(r_t_ok, 1)
            for j in range(2):
                dve.wait_ge(s_hi_ok, 2 * n + j + 1)
                dve.tensor_tensor(s_lo[j][:, :, 0:NPB], spread(turn_bank[j]), s_hi[j][:, :, 0:NPB].bitcast(F32),
                                  ALU.subtract).then_inc(s_lo_ok, 1)

        def low_hidden(n):
            dve.wait_ge(nt_hi_ok, n + 1)
            need(dve, node_mm, n)
            dve.tensor_tensor(nt_lo[:, :, 0:NPB], spread(hturn_bank), nt_hi[:, :, 0:NPB].bitcast(F32),
                              ALU.subtract).then_inc(nt_lo_ok, 1)

        def norms(n, u):
            at = [0]

            def done(ins):
                at[0] += 1
                ins.then_inc(y_step, 1)
                dve.wait_ge(y_step, n * STEPS + at[0])

            dve.wait_ge(node_mm, n + 1)
            need(dve, final_ok, n)
            done(dve.tensor_tensor(y[:], node_bank[0:NPB, :], b1[:], ALU.add))
            done(dve.bn_stats(stats[:, 0:6], y[:]))
            dve.sem_inc(tick, 1)
            done(dve.bn_aggr(moments[:, 0:2], stats[:, 0:6]))
            dve.tensor_scalar(dev[:, 0:1], moments[:, 1:2], EPS, None, ALU.add).then_inc(var_ok, 1)
            done(dve.scalar_tensor_tensor(out=y[:], in0=y[:], scalar=moments[:, 0:1], in1=gain[:],
                                          op0=ALU.subtract, op1=ALU.mult))
            dve.wait_ge(dev_ok, 2 * n + 1)
            dve.wait_ge(x2_ok, n + 1)
            done(dve.scalar_tensor_tensor(out=y[:], in0=y[:], scalar=dev[:, 1:2], in1=x2[u][:],
                                          op0=ALU.mult, op1=ALU.add))
            done(dve.bn_stats(stats[:, 0:6], y[:]))
            dve.sem_inc(tick, 1)
            done(dve.bn_aggr(moments[:, 0:2], stats[:, 0:6]))
            dve.tensor_scalar(dev[:, 0:1], moments[:, 1:2], EPS, None, ALU.add).then_inc(var_ok, 1)
            dve.wait_ge(dev_ok, 2 * n + 2)
            if not (isinstance(n, int) and n < 2):
                dve.wait_ge(stored[u], (n - u) * 8)
            dve.tensor_scalar(final[u][:], y[:], moments[:, 0:1], dev[:, 1:2], ALU.subtract, ALU.mult).then_inc(final_ok, 1)
            assert at[0] == STEPS

        def tiles(i):
            for u in range(2):
                n = 2 * i + u
                if exists(n - 1):
                    low_hidden(n - 1)
                if exists(n - 2):
                    norms(n - 2, u)
                dve.wait_ge(hidden_mm, n + 1)
                dve.wait_ge(tile_in[u], (n - u) * 8 + 16)
                need(dve, hidden_ok, n - 1)
                dve.tensor_tensor(added[u][:], hidden_bank[0:NPB, :], own[u][:], ALU.add).then_inc(own_ok, 1)
                if not (isinstance(n, int) and n == NB - 1):
                    low_sums(n + 1)

        low_sums(0)
        for i in range(3):
            dve.wait_ge(mat_hi_ok, i + 1)
            dve.tensor_tensor(m_lo[i][:], m_f[i][:], m_hi[i][:].bitcast(F32), ALU.subtract).then_inc(mat_ok, 1)
        dve.wait_ge(row_in, 144)
        pairs(dve, tiles)
        low_hidden(NB - 1)
        norms(NB - 2, 0)
        norms(NB - 1, 1)

    @block.scalar
    def _(act):

        def copy_sums(n, u):
            need(act, turned, 2 * (n - 1))
            need(act, r_turned, n - 1)
            for j, s in enumerate((k["sum_p"], k["sum_h"])):
                act.activation(s_in[j][u][:], tile_of(s, n)[0:NPB, :], ACT.Copy)
            act.activation(r_in[u][:], tile_of(k["sum_r"], n)[0:NPB, :], ACT.Copy).then_inc(copied, 1)

        def high_sums(n):
            need(act, hidden_mm, n)
            for j in range(2):
                act.wait_ge(turned, 2 * n + j + 1)
                act.activation(s_hi[j][:, :, 0:NPB], spread(turn_bank[j]), ACT.Copy).then_inc(s_hi_ok, 1)

        copy_sums(0, 0)
        high_sums(0)
        for i in range(3):
            act.activation(m_hi[i][:], m_f[i][:], ACT.Copy).then_inc(mat_hi_ok, 1)

        def high_hidden(n):
            act.wait_ge(hidden_turned, n + 1)
            need(act, node_mm, n)
            act.activation(nt_hi[:, :, 0:NPB], spread(hturn_bank), ACT.Copy).then_inc(nt_hi_ok, 1)

        def tiles(i):
            for u in range(2):
                n = 2 * i + u
                last = isinstance(n, int) and n == NB - 1
                if exists(n - 1):
                    high_hidden(n - 1)
                if not last:
                    copy_sums(n + 1, 1 - u)
                act.wait_ge(own_ok, n + 1)
                need(act, hidden_turned, n - 1)
                act.activation(hidden[u][:], added[u][:], ACT.Silu).then_inc(hidden_ok, 1)
                if not last:
                    high_sums(n + 1)

        pairs(act, tiles)
        high_hidden(NB - 1)

    @block.tensor
    def _(pe):
        def turn_sums(n, u):
            pe.wait_ge(copied, n + 1)
            need(pe, s_lo_ok, 2 * n)
            need(pe, r_t_ok, n)
            for j in range(2):
                for c in range(KC):
                    last = pe.transpose(turn_bank[j][:, c * P:c * P + NPB], s_in[j][u][:, c * P:(c + 1) * P], k["ident"][0:NPB, 0:NPB])
                last.then_inc(turned, 1)
            pe.matmul(small_bank[0:8, 0:NPB], r_in[u][:], k["ident"][0:NPB, 0:NPB], start=True, stop=True).then_inc(r_turned, 1)

        def turn_hidden(n, u):
            pe.wait_ge(hidden_ok, n + 1)
            need(pe, nt_lo_ok, n)
            for c in range(KC):
                last = pe.transpose(hturn_bank[:, c * P:c * P + NPB], hidden[u][:, c * P:(c + 1) * P], k["ident"][0:NPB, 0:NPB])
            last.then_inc(hidden_turned, 1)

        def second(n):
            if isinstance(n, int) and n == 0:
                pe.wait_ge(mat_ok, 3)
            pe.wait_ge(nt_lo_ok, n + 1)
            need(pe, y_step, (n - 1) * STEPS + 1)
            product(pe, node_bank[0:NPB, :], (lambda c: nt_hi[:, c, 0:NPB], lambda c: nt_lo[:, c, 0:NPB]),
                    (lambda c: m_hi[2][:, c, :], lambda c: m_lo[2][:, c, :]), range(KC)).then_inc(node_mm, 1)

        def tiles(i):
            for u in range(2):
                n = 2 * i + u
                if exists(n - 1):
                    turn_hidden(n - 1, 1 - u)
                pe.wait_ge(s_lo_ok, 2 * n + 2)
                pe.wait_ge(r_t_ok, n + 1)
                need(pe, own_ok, n)
                out = hidden_bank[0:NPB, :]
                pe.matmul(out, r_t[:], row_fold[:], start=True, stop=False, skip_group_check=True)
                for j in range(2):
                    for c in range(KC):
                        pe.matmul(out, s_hi[j][:, c, 0:NPB], m_hi[j][:, c, :], start=False, stop=False, skip_group_check=True)
                        pe.matmul(out, s_hi[j][:, c, 0:NPB], m_lo[j][:, c, :], start=False, stop=False, skip_group_check=True)
                        last = pe.matmul(out, s_lo[j][:, c, 0:NPB], m_hi[j][:, c, :], start=False,
                                         stop=(j == 1 and c == KC - 1), skip_group_check=True)
                last.then_inc(hidden_mm, 1)
                if not (isinstance(n, int) and n == NB - 1):
                    turn_sums(n + 1, 1 - u)
                if exists(n - 1):
                    second(n - 1)

        turn_sums(0, 0)
        pe.wait_ge(mat_ok, 2)
        pe.wait_ge(row_in, 144)
        pairs(pe, tiles)
        turn_hidden(NB - 1, 1)
        second(NB - 1)


SCRATCH = {"records": (P * TILES, REC), "mesh_table": (N, D), "dst_table": (N, D), "x1": (N, D), "node_own": (N, D),
           "square1": (D, D), "fold_edge": (D, D), "square2": (D, D), "fold_node1": (D, D), "fold_node2": (D, D),
           "lin1": (D,), "fold_edge_b": (D,), "lin2": (D,), "edge_shift": (D,), "node_r1": (D,), "node_r2": (D,),
           "node_count": (D,)}
KEEP = {"ident": ([P, P], F32), "grid": ([P, P], F32), "half": ([P, 1], F32), "zeros": ([P, 16], F32),
        "floor": ([P, 2], F32), "recs": ([P, TILES, REC], F32),
        "tile_last": ([P, TILES], I32), "tile_bucket1": ([P, TILES], I32),
        "bucket_end": ([P, NB], I32)}
KEEP_AB = {"adj": ([P, NB, NB * P], I16), "degree": ([P, NB], F32), "h": ([NPB, NB, D], F32),
           "w0": ([P, KC, D], F32), "w1": ([P, KC, D], F32)}
KEEP_CD = {"sum_p": ([P, NB, D], F32), "sum_h": ([P, NB, D], F32), "sum_r": ([P, NB, 8], F32),
           **{f"node_mat{i}": ([P, KC, D], F32) for i in range(3)}}


def build(nc, t, outs):
    with ExitStack() as whole:
        scratch = {n: nc.dram_tensor("s_" + n, list(s), F32, kind="Internal").ap() for n, s in SCRATCH.items()}
        keep = {n: whole.enter_context(nc.sbuf_tensor("k_" + n, s, d)) for n, (s, d) in KEEP.items()}
        with ExitStack() as both:
            keep.update({n: both.enter_context(nc.sbuf_tensor("k_" + n, s, d)) for n, (s, d) in KEEP_AB.items()})
            for phase in (phase_a, phase_b):
                with ExitStack() as ctx:
                    phase(nc, ctx, t, scratch, keep)
        keep.update({n: whole.enter_context(nc.sbuf_tensor("k_" + n, s, d)) for n, (s, d) in KEEP_CD.items()})
        with ExitStack() as ctx:
            phase_c(nc, ctx, t, scratch, keep)
        with ExitStack() as ctx:
            phase_d(nc, ctx, t, scratch, keep, outs[0])


_OUTS = [((N, D), "float32")]


def kernel(**inputs):
    import numpy as _np
    import concourse.bacc as _bacc
    from concourse import mybir as _mybir
    from concourse.bass_utils import run_bass_kernel_spmd as _run

    nc = _bacc.Bacc("TRN2", target_bir_lowering=False, num_devices=1)
    arrays, tensors, outs = {}, {}, []
    for name, a in inputs.items():
        a = _np.ascontiguousarray(a)
        arrays[f"in_{name}_dram"] = a
        tensors[name] = nc.dram_tensor(f"in_{name}_dram", a.shape, _mybir.dt.from_np(a.dtype), kind="ExternalInput").ap()
    for i, (shape, dtype) in enumerate(_OUTS):
        dt = _mybir.dt.from_np(_np.dtype(dtype))
        outs.append(nc.dram_tensor(f"out_{i}_dram", shape, dt, kind="ExternalOutput").ap())
    build(nc, tensors, outs)
    r = _run(nc, [arrays], core_ids=[0])
    got = tuple(r.results[0][f"out_{i}_dram"] for i in range(len(_OUTS)))
    return got if len(got) > 1 else got[0]
```
